# Optimizing a Trainium2 kernel written in Bass

```python
import numpy as np
import jax
import jax.numpy as jnp

def _softmax(x, axis=-1):
    return jax.nn.softmax(x, axis=axis)

def _gelu(x):
    return jax.nn.gelu(x, approximate=True)

def _silu(x):
    return jax.nn.silu(x)

def _sigmoid(x):
    return jax.nn.sigmoid(x)

def _layernorm(x, axis=-1, eps=1e-05):
    m = jnp.mean(x, axis=axis, keepdims=True)
    v = jnp.var(x, axis=axis, keepdims=True)
    return (x - m) / jnp.sqrt(v + eps)

def _scatter_add(tgt, idx, src, axis=0):
    return tgt.at[idx].add(src)

def _segment_sum(src, seg, n):
    return jax.ops.segment_sum(src, seg, n)
kernel_name = 'mk_flamingo_gated_d1_seqx_r4_e1a205'

def setup_inputs(seed: int=0):
    np.random.seed(seed)
    _w = jnp.asarray

    def _rec_inputs():
        import jax
        import jax.numpy as jnp
        _rk = jax.random.key(seed)
        x = 7.22e-05 + 1 * jax.random.normal(jax.random.fold_in(_rk, 1), (128, 128, 256), jnp.float32)
        _lenS = 128 - jax.random.randint(jax.random.fold_in(_rk, 7), (128,), 0, max(1, 128 // 4) + 1, jnp.int32)
        _lenS2 = 128 - jax.random.randint(jax.random.fold_in(_rk, 8), (128,), 0, max(1, 128 // 4) + 1, jnp.int32)
        _ctx_1024P = jax.random.normal(jax.random.fold_in(_rk, 11), (128, 16, 256), jnp.float32)
        _ctx_1024c = jax.random.dirichlet(jax.random.fold_in(_rk, 511), 0.3 * jnp.ones((16,), jnp.float32), (128, 128))
        _ctx_1024t = jnp.einsum('bsk,bkd->bsd', _ctx_1024c, _ctx_1024P)
        _ctx_1024t = _ctx_1024t * jax.lax.rsqrt(jnp.mean(jnp.square(_ctx_1024t)) + 1e-12) * 0.953939
        ctx_1024 = 4.13588e-05 + 0.999923 * (_ctx_1024t + 0.3 * jax.random.normal(jax.random.fold_in(_rk, 611), (128, 128, 256), jnp.float32))
        _g = jax.random.normal(jax.random.fold_in(_rk, 9001), (2, 1), jnp.float32)
        _g = jnp.sign(_g) * jnp.maximum(jnp.abs(_g), 1.0) + (_g == 0) * 1.0
        g_xattn = _g[0]
        g_ffn = _g[1]
        return (x, ctx_1024, g_xattn, g_ffn)
    x, ctx_1024, g_xattn, g_ffn = _rec_inputs()

    def _L0_xattn_setup():
        import jax, jax.numpy as jnp
        import numpy as np
        import math
        DIM = 256
        HEADS = 16
        WINDOW = 64

        def _rope(x):
            b, s, d = x.shape
            half = d // 2
            inv_freq = 1.0 / 10000.0 ** (jnp.arange(half, dtype=jnp.float32) / half)
            ang = jnp.arange(s, dtype=jnp.float32)[:, None] * inv_freq[None, :]
            cos, sin = (jnp.cos(ang), jnp.sin(ang))
            x1, x2 = (x[..., :half], x[..., half:])
            return jnp.concatenate([x1 * cos - x2 * sin, x1 * sin + x2 * cos], axis=-1)
        key = jax.random.key(seed)
        ks = jax.random.split(key, 8)
        d = DIM
        q = jax.random.normal(ks[0], (2, 1024, d), dtype=jnp.float32)
        k = jax.random.normal(ks[1], (2, 1024, d), dtype=jnp.float32)
        v = jax.random.normal(ks[2], (2, 1024, d), dtype=jnp.float32)
        wq = jax.random.normal(ks[3], (d, d), dtype=jnp.float32) * 0.02
        wk = jax.random.normal(ks[4], (d, d), dtype=jnp.float32) * 0.02
        wv = jax.random.normal(ks[5], (d, d), dtype=jnp.float32) * 0.02
        wo_w = jax.random.normal(ks[6], (d, d), dtype=jnp.float32) * 0.02
        wo_b = jnp.zeros((d,), dtype=jnp.float32)
        return {'q': q, 'k': k, 'v': v, 'wq': wq, 'wk': wk, 'wv': wv, 'wo_w': wo_w, 'wo_b': wo_b}
    _L0_xattn_all = _L0_xattn_setup()
    _L0_xattn_in = {k: v for k, v in _L0_xattn_all.items() if k in ('wq', 'wk', 'wv', 'wo_w', 'wo_b')}
    del _L0_xattn_all

    def _L0_ffn_setup():
        import jax, jax.numpy as jnp
        import numpy as np
        E = 16
        K = 2
        LOAD = 1.0

        def _dispatch(xb, pb, cap):
            T, C = xb.shape
            top_k_probs, ei = jax.lax.top_k(pb, K)
            flat = ei.swapaxes(0, 1).ravel()
            one_hot = jax.nn.one_hot(flat, E, dtype=jnp.int32)
            pos = jnp.cumsum(one_hot, axis=0) * one_hot
            pos = pos.reshape(K, T, E).swapaxes(0, 1)
            pos = jnp.max(pos, axis=-1) - 1
            ei2 = flat.reshape(K, T).swapaxes(0, 1)
            xr = jnp.repeat(xb, K, axis=0)
            buf = jnp.zeros((E, cap, C), xb.dtype)
            buf = buf.at[ei2.ravel(), pos.ravel()].set(xr, mode='drop')
            return (top_k_probs, pos, ei2, buf)

        def _collect(eo_b, ei_b, pos_b, tk_b):
            out = eo_b[ei_b, pos_b]
            return jnp.sum(tk_b[..., None] * out, axis=1)
        key = jax.random.key(seed)
        k1, k2, k3, k4, k5 = jax.random.split(key, 5)
        B, T, C, H = (8, 1024, 256, 128)
        n_layer = 12
        x = jax.random.normal(k1, (B, T, C), dtype=jnp.float32)
        w_router = jax.random.normal(k2, (C, E), dtype=jnp.float32) * 0.02
        w_fc = jax.random.normal(k3, (E, C, H), dtype=jnp.float32) * 0.02
        w_gate = jax.random.normal(k4, (E, C, H), dtype=jnp.float32) * 0.02
        w_proj = jax.random.normal(k5, (E, H, C), dtype=jnp.float32) * (0.02 * (2 * n_layer) ** (-0.5))
        return {'x': x, 'w_router': w_router, 'w_fc': w_fc, 'w_gate': w_gate, 'w_proj': w_proj}
    _L0_ffn_all = _L0_ffn_setup()
    _L0_ffn_in = {k: v for k, v in _L0_ffn_all.items() if k in ('w_router', 'w_fc', 'w_gate', 'w_proj')}
    del _L0_ffn_all
    return {'x': x, 'ctx_1024': ctx_1024, 'g_xattn': g_xattn, 'g_ffn': g_ffn, 'L0_xattn_wq': _L0_xattn_in['wq'], 'L0_xattn_wk': _L0_xattn_in['wk'], 'L0_xattn_wv': _L0_xattn_in['wv'], 'L0_xattn_wo_w': _L0_xattn_in['wo_w'], 'L0_xattn_wo_b': _L0_xattn_in['wo_b'], 'L0_ffn_w_router': _L0_ffn_in['w_router'], 'L0_ffn_w_fc': _L0_ffn_in['w_fc'], 'L0_ffn_w_gate': _L0_ffn_in['w_gate'], 'L0_ffn_w_proj': _L0_ffn_in['w_proj']}

def reference(x, ctx_1024, g_xattn, g_ffn, L0_xattn_wq, L0_xattn_wk, L0_xattn_wv, L0_xattn_wo_w, L0_xattn_wo_b, L0_ffn_w_router, L0_ffn_w_fc, L0_ffn_w_gate, L0_ffn_w_proj):
    import jax
    import jax.numpy as jnp

    def _L0_xattn_ref(q, k, v, wq, wk, wv, wo_w, wo_b):
        import jax, jax.numpy as jnp
        import numpy as np
        import math
        DIM = 256
        HEADS = 16
        WINDOW = 64

        def _rope(x):
            b, s, d = x.shape
            half = d // 2
            inv_freq = 1.0 / 10000.0 ** (jnp.arange(half, dtype=jnp.float32) / half)
            ang = jnp.arange(s, dtype=jnp.float32)[:, None] * inv_freq[None, :]
            cos, sin = (jnp.cos(ang), jnp.sin(ang))
            x1, x2 = (x[..., :half], x[..., half:])
            return jnp.concatenate([x1 * cos - x2 * sin, x1 * sin + x2 * cos], axis=-1)
        b, s, d = q.shape
        h, W = (HEADS, WINDOW)
        dk = d // h
        B = W
        nb = s // B
        qp = _rope(jnp.einsum('bsd,ed->bse', q, wq))
        kp = _rope(jnp.einsum('bsd,ed->bse', k, wk))
        vp = jnp.einsum('bsd,ed->bse', v, wv)
        qh = qp.reshape(b, s, h, dk).transpose(0, 2, 1, 3)
        kh = kp.reshape(b, s, h, dk).transpose(0, 2, 1, 3)
        vh = vp.reshape(b, s, h, dk).transpose(0, 2, 1, 3)
        kpad = jnp.pad(kh, ((0, 0), (0, 0), (B, B), (0, 0)))
        vpad = jnp.pad(vh, ((0, 0), (0, 0), (B, B), (0, 0)))
        kblk = kpad.reshape(b, h, nb + 2, B, dk)
        vblk = vpad.reshape(b, h, nb + 2, B, dk)
        kband = jnp.concatenate([kblk[:, :, i:i + nb] for i in range(3)], axis=3)
        vband = jnp.concatenate([vblk[:, :, i:i + nb] for i in range(3)], axis=3)
        qb = qh.reshape(b, h, nb, B, dk)
        scores = jnp.einsum('bhnqd,bhnkd->bhnqk', qb, kband) * math.sqrt(dk)
        n_idx = jnp.arange(nb)[:, None, None]
        qi = jnp.arange(B)[None, :, None]
        ki = jnp.arange(3 * B)[None, None, :]
        kpos = (n_idx - 1) * B + ki
        rel = ki - B - qi
        valid = (rel >= -W) & (rel <= W) & (kpos >= 0) & (kpos < s)
        neg = jnp.asarray(jnp.finfo(scores.dtype).min, scores.dtype)
        scores = jnp.where(valid[None, None], scores, neg)
        attn = jax.nn.softmax(scores, axis=-1)
        out = jnp.einsum('bhnqk,bhnkd->bhnqd', attn, vband)
        out = out.reshape(b, h, s, dk).transpose(0, 2, 1, 3).reshape(b, s, d)
        return jnp.einsum('bsd,ed->bse', out, wo_w) + wo_b

    def _L0_ffn_ref(x, w_router, w_fc, w_gate, w_proj):
        import jax, jax.numpy as jnp
        import numpy as np
        E = 16
        K = 2
        LOAD = 1.0

        def _dispatch(xb, pb, cap):
            T, C = xb.shape
            top_k_probs, ei = jax.lax.top_k(pb, K)
            flat = ei.swapaxes(0, 1).ravel()
            one_hot = jax.nn.one_hot(flat, E, dtype=jnp.int32)
            pos = jnp.cumsum(one_hot, axis=0) * one_hot
            pos = pos.reshape(K, T, E).swapaxes(0, 1)
            pos = jnp.max(pos, axis=-1) - 1
            ei2 = flat.reshape(K, T).swapaxes(0, 1)
            xr = jnp.repeat(xb, K, axis=0)
            buf = jnp.zeros((E, cap, C), xb.dtype)
            buf = buf.at[ei2.ravel(), pos.ravel()].set(xr, mode='drop')
            return (top_k_probs, pos, ei2, buf)

        def _collect(eo_b, ei_b, pos_b, tk_b):
            out = eo_b[ei_b, pos_b]
            return jnp.sum(tk_b[..., None] * out, axis=1)
        B, T, C = x.shape
        cap = int(LOAD * K * max(1, T / E))
        g = jnp.einsum('btc,ce->bte', x, w_router)
        gate_probs = jax.nn.softmax(g, axis=-1)
        top_k_probs, positions, indices, expert_inputs = jax.vmap(lambda xb, pb: _dispatch(xb, pb, cap))(x, gate_probs)
        expert_inputs = jnp.swapaxes(expert_inputs, 0, 1).reshape(E, B * cap, C)
        gg = jnp.einsum('enc,ech->enh', expert_inputs, w_gate)
        h = jnp.einsum('enc,ech->enh', expert_inputs, w_fc)
        h = jax.nn.silu(gg) * h
        o = jnp.einsum('enh,ehc->enc', h, w_proj)
        expert_outputs = jnp.swapaxes(o.reshape(E, B, cap, C), 0, 1)
        y = jax.vmap(_collect)(expert_outputs, indices, positions, top_k_probs)
        return y
    x = x + jnp.tanh(g_xattn[0]) * _L0_xattn_ref(_layernorm(x, axis=-1), ctx_1024, ctx_1024, L0_xattn_wq, L0_xattn_wk, L0_xattn_wv, L0_xattn_wo_w, L0_xattn_wo_b)
    x = x + jnp.tanh(g_ffn[0]) * _L0_ffn_ref(_layernorm(x, axis=-1), L0_ffn_w_router, L0_ffn_w_fc, L0_ffn_w_gate, L0_ffn_w_proj)
    return x

_drawn_inputs = setup_inputs


def setup_inputs(seed=0):
    import zlib

    import numpy as np

    out = dict(_drawn_inputs(seed))
    spreads = {'L0_xattn_wo_b': (0.0, 0.1)}
    factors = {'L0_ffn_w_router': 8.0, 'L0_ffn_w_fc': 8.0, 'L0_ffn_w_gate': 8.0, 'L0_ffn_w_proj': 8.0}
    for name, (base, spread) in spreads.items():
        noise = np.random.default_rng([zlib.crc32(name.encode()), seed]).standard_normal(out[name].shape)
        drawn = base * np.exp(spread * noise) if base else spread * noise
        out[name] = jnp.asarray(drawn.astype(out[name].dtype))
    for name, factor in factors.items():
        out[name] = (out[name] * factor).astype(out[name].dtype)
    return out
```

```python
from contextlib import ExitStack

import numpy as np

import concourse.bass as bass
from concourse import mybir

F32 = mybir.dt.float32
F32R = mybir.dt.float32r
BF16 = mybir.dt.bfloat16
ALU = mybir.AluOpType
ACT = mybir.ActivationFunctionType
AX_X = mybir.AxisListType.X

P = 128
SEQS, SEQ, DIM = 128, 128, 256
HEADS = 16
DK = DIM // HEADS
WINDOW = 64
KC = DIM // P
PAIRS = SEQS // 2
UNITS = 8
EXPERTS, TOPK, HID = 16, 2, 128
CAP = TOPK * SEQ // EXPERTS
SLOTS = EXPERTS * CAP
GROUP = P // CAP
GROUPS = SEQS // GROUP
EPS = 1e-5
FAR = float(2.0 ** 100)
GONE = 1000.0


def wait_for(eng, sem, value):
    if isinstance(value, int) and value <= 0:
        return
    eng.wait_ge(sem, value)


class Pair:

    def __init__(self, i, c):
        self.i, self.c = i, c

    def __add__(self, d):
        return Pair(self.i, self.c + d)

    def __sub__(self, d):
        return Pair(self.i, self.c - d)

    @property
    def n(self):
        return self.i * 2 + self.c

    @property
    def par(self):
        return self.c % 2

    @property
    def half(self):
        return self.i + self.c // 2

    @property
    def real(self):
        return not isinstance(self.i, int) or 0 <= self.i * 2 + self.c < PAIRS

    def landed(self):
        return (self.half + 1) * 16


def attention_block(nc, ctx, T, D):

    def sb(name, shape, dt=F32):
        return ctx.enter_context(nc.sbuf_tensor(name, shape, dt))

    def pb(name):
        return ctx.enter_context(nc.psum_tensor(name, [P, 512], F32))

    def sem(name):
        return ctx.enter_context(nc.semaphore(name))

    x_in_sb = sb("x_in_sb", [P, 2, 2, DIM])
    c_in_sb = sb("c_in_sb", [P, 2, 2, DIM])
    xr_sb = sb("xr_sb", [P, 2, 2, DIM])
    xb = sb("xb", [P, 2, DIM])
    stage = sb("stage", [P, 4, KC, DIM])
    w_hi = sb("w_hi", [P, 4, KC, DIM], F32R)
    w_lo = sb("w_lo", [P, 4, KC, DIM], F32R)
    wr = sb("wr", [P, KC, 32])
    tb = sb("tb", [P, DIM])
    cos = sb("cos_sb", [P, SEQ])
    sin = sb("sin_sb", [P, SEQ])
    band = sb("band_sb", [P, SEQ])
    kmask = sb("kmask_sb", [P, 2])
    ident = sb("ident_sb", [P, P])
    stats = sb("stats", [P, 2, 6])
    stats2 = sb("stats2", [P, 2, 6])
    mv = sb("mv", [P, 2, 2])
    mv2 = sb("mv2", [P, 2, 2])
    ve = sb("ve", [P, 2])
    ve2 = sb("ve2", [P, 2])
    rstd = sb("rstd", [P, 2])
    rstd2 = sb("rstd2", [P, 2])
    mhalf = sb("mhalf", [P, 2])
    xn = sb("xn", [P, 2, DIM])
    xt_hi = sb("xt_hi", [P, KC, 2, SEQ], F32R)
    xt_lo = sb("xt_lo", [P, KC, 2, SEQ], F32R)
    ct_hi = sb("ct_hi", [P, KC, 2, SEQ], F32R)
    ct_lo = sb("ct_lo", [P, KC, 2, SEQ], F32R)
    q_cos = sb("q_cos", [P, KC, 2 * SEQ])
    q_sin = sb("q_sin", [P, KC, 2 * SEQ])
    k_cos = sb("k_cos", [P, KC, 2 * SEQ])
    k_sin = sb("k_sin", [P, KC, 2 * SEQ])
    q_rot = sb("q_rot", [P, KC, 2 * SEQ])
    k_rot = sb("k_rot", [P, KC, 2 * SEQ])
    q_hi = sb("q_hi", [P, 2, KC, 2, SEQ], F32R)
    q_lo = sb("q_lo", [P, 2, KC, 2, SEQ], F32R)
    k_hi = sb("k_hi", [P, 2, KC, 2, 2, SEQ], F32R)
    k_lo = sb("k_lo", [P, 2, KC, 2, 2, SEQ], F32R)
    v_aug = sb("v_aug", [P, 2, 2, HEADS, 32])
    neg_s = sb("neg_s", [P, 2, 4, SEQ])
    neg_max = sb("neg_max", [P, 2, 4])
    probs = sb("probs", [P, 2, 4, SEQ])
    probs_t = sb("probs_t", [P, 2, 4, SEQ])
    out_t = sb("out_t", [P, 2, 4, SEQ])
    rden = sb("rden", [P, 2, HEADS])
    att = sb("att", [P, 2, DIM])
    at_hi = sb("at_hi", [P, KC, 2, SEQ], F32R)
    at_lo = sb("at_lo", [P, KC, 2, SEQ], F32R)
    x1 = sb("x1", [P, 2, 2, DIM])
    xn2 = sb("xn2", [P, 2, 2, DIM])
    x2t = sb("x2t", [P, KC, 2, SEQ])
    lt_sb = sb("lt_sb", [64, SEQ])
    gates = T["gates"]
    logits = T["logits"]

    S = [pb("S0"), pb("S1")]
    PT = [pb("PT0"), pb("PT1")]
    PO = pb("PO")
    F0, F1, F2 = pb("F0"), pb("F1"), pb("F2")

    names = ("consts_in wproj_in w_split gate_tanh setup_dve setup_pool tb_done "
             "ln_stats ln_aggr rstd_done ve_done xn_done xb_done "
             "tx_done tc_done xt_hi_done xt_lo_done ct_hi_done ct_lo_done qt_done kt_done v_done "
             "q_scaled k_scaled q_rotated k_rotated q_hi_done q_lo_done k_hi_done k_lo_done v_ready "
             "scores_done rowmax_done probs_done pt_done pt_copied pv_done ot_copied o2_done rden_done att_done "
             "at_done at_hi_done at_lo_done wo_done x1_done ln2_stats ln2_aggr ve2_done rstd2_done xn2_done "
             "x2t_done x2t_copied rt_done lt_copied lg_done logits_done "
             "dve_passed pe_passed").split()
    M = {n: sem(n) for n in names}
    x_in = [sem("x_in0"), sem("x_in1")]
    c_in = [sem("c_in0"), sem("c_in1")]
    xr_in = [sem("xr_in0"), sem("xr_in1")]
    x1_out = [sem("x1_out0"), sem("x1_out1")]
    xn2_out = [sem("xn2_out0"), sem("xn2_out1")]

    def run(eng, step):
        for c in range(-3, 2):
            step(Pair(0, c))
        with eng.Fori(1, PAIRS // 2 - 2) as i:
            step(Pair(i, 0))
            step(Pair(i, 1))
        for c in range(PAIRS - 4, PAIRS + 2):
            step(Pair(0, c))

    block = ctx.enter_context(nc.Block())

    @block.sync
    def _(sp):
        for k, name in enumerate(("wq", "wk", "wv", "wo")):
            sp.dma_start(stage[:, k], D[name].rearrange("(k p) e -> p k e", p=P)).then_inc(M["wproj_in"], 16)
        for dst, name in ((cos, "cos"), (sin, "sin"), (band, "band"), (kmask, "kmask"), (ident, "ident")):
            sp.dma_start(dst[:], D[name]).then_inc(M["consts_in"], 16)
        sp.dma_start(wr[:, :, 0:EXPERTS], D["w_router"].rearrange("(k p) e -> p k e", p=P)).then_inc(M["consts_in"], 16)
        sp.dma_start(tb[:], D["wo_b"].partition_broadcast(P)).then_inc(M["consts_in"], 16)
        sp.dma_start(gates[:, 0:1], D["g_xattn"].partition_broadcast(P)).then_inc(M["consts_in"], 16)
        sp.dma_start(gates[:, 1:2], D["g_ffn"].partition_broadcast(P)).then_inc(M["consts_in"], 16)

        def step(s):
            n = s + 3
            if n.real:
                wait_for(sp, M["xn_done"], (n - 1).n)
                sp.dma_start(x_in_sb[:, n.par], D["x"][bass.ds(n.n * 2, 2)].rearrange("b t c -> t b c")) \
                    .then_inc(x_in[n.par], 16)
            n = s + 2
            if n.real:
                wait_for(sp, M["tc_done"], (n - 1).n)
                sp.dma_start(c_in_sb[:, n.par], D["ctx"][bass.ds(n.n * 2, 2)].rearrange("b t c -> t b c")) \
                    .then_inc(c_in[n.par], 16)
            n = s
            if n.real:
                wait_for(sp, M["xb_done"], (n - 1).n)
                sp.dma_start(xr_sb[:, n.par], D["x"][bass.ds(n.n * 2, 2)].rearrange("b t c -> t b c")) \
                    .then_inc(xr_in[n.par], 16)
            n = s - 2
            if n.real:
                sp.wait_ge(M["x1_done"], (n + 1).n)
                sp.dma_start(D["x1_d"][:, bass.ds(n.n * 2, 2)], x1[:, n.par]).then_inc(x1_out[n.par], 16)
                sp.wait_ge(M["xn2_done"], (n + 1).n)
                sp.dma_start(D["xn2_d"][:, bass.ds(n.n * 2, 2)], xn2[:, n.par]).then_inc(xn2_out[n.par], 16)

        run(sp, step)
        for q in x1_out + xn2_out:
            sp.wait_ge(q, 16 * (PAIRS // 2))

    @block.gpsimd
    def _(pool):
        pool.memset(mhalf[:], -0.5).then_inc(M["setup_pool"], 1)
        pool.memset(v_aug[:, :, :, :, DK:32], 1.0).then_inc(M["setup_pool"], 1)
        pool.wait_ge(M["setup_pool"], 2)
        pool.wait_ge(M["tb_done"], 1)

        def step(s):
            n = s - 1
            if n.real:
                pool.wait_ge(xr_in[n.par], n.landed())
                wait_for(pool, M["x1_done"], n.n)
                for b in range(2):
                    last = pool.tensor_tensor(xb[:, b], xr_sb[:, n.par, b], tb[:], ALU.add)
                last.then_inc(M["xb_done"], 1)
            n = s + 2
            if n.real:
                pool.wait_ge(M["ve_done"], (n + 1).n)
                wait_for(pool, M["xn_done"], n.n)
                pool.tensor_tensor(rstd[:], ve[:], mhalf[:], ALU.pow).then_inc(M["rstd_done"], 1)
            n = s + 1
            if n.real:
                for qc, qs, rot, scaled, rotated, split in (
                        (q_cos, q_sin, q_rot, "q_scaled", "q_rotated", ("q_hi_done", "q_lo_done")),
                        (k_cos, k_sin, k_rot, "k_scaled", "k_rotated", ("k_hi_done", "k_lo_done"))):
                    pool.wait_ge(M[scaled], (n + 1).n)
                    for done in split:
                        wait_for(pool, M[done], n.n)
                    pool.tensor_tensor(rot[:, 0], qc[:, 0], qs[:, 1], ALU.subtract)
                    pool.tensor_tensor(rot[:, 1], qc[:, 1], qs[:, 0], ALU.add).then_inc(M[rotated], 1)
                pool.wait_ge(M["q_hi_done"], (n + 1).n)
                wait_for(pool, M["scores_done"], (n - 1).n * UNITS)
                pool.wait_ge(M["q_rotated"], (n + 1).n)
                pool.tensor_tensor(q_lo[:, n.par].rearrange("p k b t -> p (k b t)"),
                                   q_rot[:].rearrange("p k t -> p (k t)"),
                                   q_hi[:, n.par].rearrange("p k b t -> p (k b t)").bitcast(F32), ALU.subtract) \
                    .then_inc(M["q_lo_done"], 1)
            n = s - 1
            if n.real:
                pool.wait_ge(M["ve2_done"], (n + 1).n)
                wait_for(pool, M["xn2_done"], n.n)
                pool.tensor_tensor(rstd2[:], ve2[:], mhalf[:], ALU.pow).then_inc(M["rstd2_done"], 1)

        run(pool, step)

    @block.scalar
    def _(act):
        act.wait_ge(M["consts_in"], 16 * 9)
        act.activation(gates[:, 2:4], gates[:, 0:2], ACT.Tanh).then_inc(M["gate_tanh"], 1)
        act.wait_ge(M["wproj_in"], 64)
        act.activation(w_hi[:].rearrange("p a k e -> p (a k e)"), stage[:].rearrange("p a k e -> p (a k e)"), ACT.Copy) \
            .then_inc(M["w_split"], 1)

        def exp_unit(n, u):
            U = n.n * UNITS + u
            act.wait_ge(M["rowmax_done"], U + 1)
            wait_for(act, M["pt_done"], U - 1)
            for j in range(4):
                last = act.activation(probs[:, u % 2, j], neg_s[:, u % 2, j], ACT.Exp,
                                      bias=neg_max[:, u % 2, j:j + 1], scale=-1.0)
            last.then_inc(M["probs_done"], 1)

        def copy_unit(n, u):
            U = n.n * UNITS + u
            act.wait_ge(M["pt_done"], U + 1)
            wait_for(act, M["pv_done"], U - 1)
            act.activation(probs_t[:, u % 2].rearrange("p j q -> p (j q)"), PT[u % 2][:], ACT.Copy) \
                .then_inc(M["pt_copied"], 1)

        def copy_out_t(n, b):
            act.wait_ge(M["pv_done"], n.n * UNITS + 4 * b + 4)
            wait_for(act, M["o2_done"], n.n * 2 + b - 1)
            act.activation(out_t[:, b].rearrange("p i q -> p (i q)"), PO[:], ACT.Copy).then_inc(M["ot_copied"], 1)

        def step(s):
            for k in range(UNITS):
                n, u = (s, k - 1) if k else (s - 1, UNITS - 1)
                if n.real:
                    exp_unit(n, u)
                n, u = (s, k - 2) if k >= 2 else (s - 1, k + UNITS - 2)
                if n.real:
                    copy_unit(n, u)
                n = s + 1
                if k == 0 and n.real:
                    wait_for(act, M["v_done"], n.n)
                    act.wait_ge(M["tx_done"], (n + 1).n)
                    act.activation(xt_hi[:].rearrange("p k b t -> p (k b t)"), F0[:], ACT.Copy) \
                        .then_inc(M["xt_hi_done"], 1)
                    act.wait_ge(M["tc_done"], (n + 1).n)
                    act.activation(ct_hi[:].rearrange("p k b t -> p (k b t)"), F1[:], ACT.Copy) \
                        .then_inc(M["ct_hi_done"], 1)
                if k == 0 and (s - 2).real:
                    n = s - 2
                    act.wait_ge(M["x2t_done"], (n + 1).n)
                    wait_for(act, M["rt_done"], n.n)
                    act.activation(x2t[:].rearrange("p k b t -> p (k b t)"), F2[:], ACT.Copy) \
                        .then_inc(M["x2t_copied"], 1)
                if k == 1 and (s - 2).real:
                    n = s - 2
                    act.wait_ge(M["rt_done"], (n + 1).n)
                    wait_for(act, M["lg_done"], n.n)
                    act.activation(lt_sb[:], F2[0:64, 0:SEQ], ACT.Copy).then_inc(M["lt_copied"], 1)
                if k == 2 and (s - 1).real:
                    copy_out_t(s - 1, 1)
                n = s + 1
                if k == 4 and n.real:
                    wait_for(act, M["scores_done"], (n - 1).n * UNITS)
                    act.wait_ge(M["q_rotated"], (n + 1).n)
                    act.activation(q_hi[:, n.par].rearrange("p k b t -> p (k b t)"),
                                   q_rot[:].rearrange("p k t -> p (k t)"), ACT.Copy).then_inc(M["q_hi_done"], 1)
                    act.wait_ge(M["k_rotated"], (n + 1).n)
                    for e in range(2):
                        last = act.activation(k_hi[:, n.par, :, :, e].rearrange("p k b t -> p (k b) t"),
                                              k_rot[:].rearrange("p k (b t) -> p (k b) t", b=2),
                                              ACT.Copy, scale=kmask[:, e:e + 1])
                    last.then_inc(M["k_hi_done"], 1)
                if k == 5 and n.real:
                    act.wait_ge(M["v_done"], (n + 1).n)
                    act.wait_ge(M["setup_pool"], 2)
                    wait_for(act, M["pv_done"], (n - 1).n * UNITS)
                    act.activation(v_aug[:, n.par, :, :, 0:DK].rearrange("p b h d -> p (b h) d"),
                                   F0[:].rearrange("p (h d) -> p h d", d=DK), ACT.Copy).then_inc(M["v_ready"], 1)
                if k == 5 and (s - 1).real:
                    n = s - 1
                    act.wait_ge(M["at_done"], (n + 1).n)
                    wait_for(act, M["wo_done"], n.n)
                    act.activation(at_hi[:].rearrange("p k b t -> p (k b t)"), F1[:], ACT.Copy) \
                        .then_inc(M["at_hi_done"], 1)
                if k == 6 and s.real:
                    copy_out_t(s, 0)

        run(act, step)

    @block.vector
    def _(dve):
        dve.memset(wr[:, :, EXPERTS:32], 0.0).then_inc(M["setup_dve"], 1)
        dve.wait_ge(M["gate_tanh"], 1)
        dve.tensor_scalar(tb[:], tb[:], gates[:, 2:3], None, ALU.mult).then_inc(M["tb_done"], 1)
        dve.wait_ge(M["w_split"], 1)
        dve.tensor_tensor(w_lo[:].rearrange("p a k e -> p (a k e)"), stage[:].rearrange("p a k e -> p (a k e)"),
                          w_hi[:].rearrange("p a k e -> p (a k e)").bitcast(F32), ALU.subtract).then_inc(M["w_split"], 1)

        def row_max(n, u):
            U = n.n * UNITS + u
            dve.wait_ge(M["scores_done"], U + 1)
            wait_for(dve, M["probs_done"], U - 1)
            dve.sem_inc(M["dve_passed"], 1)
            for j in range(4):
                last = dve.tensor_tensor_reduce(neg_s[:, u % 2, j], S[u % 2][:, j * SEQ:(j + 1) * SEQ], band[:],
                                                1.0, 3e38, ALU.add, ALU.min, neg_max[:, u % 2, j:j + 1])
            last.then_inc(M["rowmax_done"], 1)

        def normalise(n, b):
            dve.wait_ge(M["o2_done"], n.n * 2 + b + 1)
            wait_for(dve, M["at_done"], n.n)
            o2 = F2[:].rearrange("p (h d) -> p h d", d=32)
            dve.reciprocal(rden[:, b], o2[:, :, DK]).then_inc(M["rden_done"], 1)
            dve.wait_ge(M["rden_done"], n.n * 2 + b + 1)
            dve.tensor_tensor(att[:, b].rearrange("p (h d) -> p h d", d=DK), o2[:, :, 0:DK],
                              rden[:, b].rearrange("p (h o) -> p h o", o=1).broadcast_to([P, HEADS, DK]), ALU.mult) \
                .then_inc(M["att_done"], 1)

        def step(s):
            for k in range(UNITS):
                if s.real:
                    row_max(s, k)
                n = s + 1
                if k == 0 and n.real:
                    for hi, lo, F, a in ((xt_hi, xt_lo, F0, "xt"), (ct_hi, ct_lo, F1, "ct")):
                        dve.wait_ge(M[a + "_hi_done"], (n + 1).n)
                        dve.tensor_tensor(lo[:].rearrange("p k b t -> p (k b t)"), F[:],
                                          hi[:].rearrange("p k b t -> p (k b t)").bitcast(F32), ALU.subtract) \
                            .then_inc(M[a + "_lo_done"], 1)
                if k == 1 and (s + 2).real:
                    n = s + 2
                    dve.wait_ge(x_in[n.par], n.landed())
                    for b in range(2):
                        last = dve.bn_stats(stats[:, b], x_in_sb[:, n.par, b])
                    last.then_inc(M["ln_stats"], 1)
                    dve.wait_ge(M["ln_stats"], (n + 1).n)
                    dve.sem_inc(M["dve_passed"], 1)
                    for b in range(2):
                        last = dve.bn_aggr(mv[:, b], stats[:, b])
                    last.then_inc(M["ln_aggr"], 1)
                    dve.wait_ge(M["ln_aggr"], (n + 1).n)
                    wait_for(dve, M["rstd_done"], n.n)
                    dve.tensor_scalar_add(ve[:], mv[:, :, 1], EPS).then_inc(M["ve_done"], 1)
                for kk, F, qc, qs, a in ((2, F0, q_cos, q_sin, "q"), (3, F1, k_cos, k_sin, "k")):
                    n = s + 1
                    if k == kk and n.real:
                        dve.wait_ge(M[a + "t_done"], (n + 1).n)
                        wait_for(dve, M[a + "_rotated"], n.n)
                        for dst, table in ((qc, cos), (qs, sin)):
                            last = dve.tensor_tensor(
                                dst[:].rearrange("p k (b t) -> p (k b) t", b=2),
                                F[:].rearrange("p (a t) -> p a t", t=SEQ),
                                table[:].rearrange("p (o t) -> p o t", o=1).broadcast_to([P, 4, SEQ]), ALU.mult)
                        last.then_inc(M[a + "_scaled"], 1)
                if k == 2 and (s - 2).real:
                    n = s - 2
                    dve.wait_ge(M["lg_done"], (n + 1).n)
                    dve.tensor_copy(logits[:, bass.ds(n.n * 2, 2), :],
                                    F2[:, 256:320].rearrange("p (b e) -> p b e", e=32)[:, :, 0:EXPERTS]) \
                        .then_inc(M["logits_done"], 1)
                if k == 3 and (s - 1).real:
                    normalise(s - 1, 1)
                n = s + 1
                if k == 5 and n.real:
                    dve.wait_ge(M["k_hi_done"], (n + 1).n)
                    for e in range(2):
                        last = dve.scalar_tensor_tensor(
                            out=k_lo[:, n.par, :, :, e].rearrange("p k b t -> p (k b) t"),
                            in0=k_rot[:].rearrange("p k (b t) -> p (k b) t", b=2), scalar=kmask[:, e:e + 1],
                            in1=k_hi[:, n.par, :, :, e].rearrange("p k b t -> p (k b) t").bitcast(F32),
                            op0=ALU.mult, op1=ALU.subtract)
                    last.then_inc(M["k_lo_done"], 1)
                if k == 5 and (s - 1).real:
                    n = s - 1
                    dve.wait_ge(M["at_hi_done"], (n + 1).n)
                    dve.tensor_tensor(at_lo[:].rearrange("p k b t -> p (k b t)"), F1[:],
                                      at_hi[:].rearrange("p k b t -> p (k b t)").bitcast(F32), ALU.subtract) \
                        .then_inc(M["at_lo_done"], 1)
                if k == 6 and (s + 2).real:
                    n = s + 2
                    dve.wait_ge(M["rstd_done"], (n + 1).n)
                    wait_for(dve, M["tx_done"], n.n)
                    for b in range(2):
                        last = dve.tensor_scalar(xn[:, b], x_in_sb[:, n.par, b], mv[:, b, 0:1], rstd[:, b:b + 1],
                                                 ALU.subtract, ALU.mult)
                    last.then_inc(M["xn_done"], 1)
                if k == 6 and (s - 1).real:
                    n = s - 1
                    dve.wait_ge(M["wo_done"], (n + 1).n)
                    dve.wait_ge(M["xb_done"], (n + 1).n)
                    wait_for(dve, x1_out[n.par], (n - 2).landed())
                    dve.scalar_tensor_tensor(out=x1[:, n.par].rearrange("p b c -> p (b c)"), in0=F0[:],
                                             scalar=gates[:, 2:3], in1=xb[:].rearrange("p b c -> p (b c)"),
                                             op0=ALU.mult, op1=ALU.add).then_inc(M["x1_done"], 1)
                    dve.wait_ge(M["x1_done"], (n + 1).n)
                    for b in range(2):
                        last = dve.bn_stats(stats2[:, b], x1[:, n.par, b])
                    last.then_inc(M["ln2_stats"], 1)
                    dve.wait_ge(M["ln2_stats"], (n + 1).n)
                    dve.sem_inc(M["dve_passed"], 1)
                    for b in range(2):
                        last = dve.bn_aggr(mv2[:, b], stats2[:, b])
                    last.then_inc(M["ln2_aggr"], 1)
                    dve.wait_ge(M["ln2_aggr"], (n + 1).n)
                    wait_for(dve, M["rstd2_done"], n.n)
                    dve.tensor_scalar_add(ve2[:], mv2[:, :, 1], EPS).then_inc(M["ve2_done"], 1)
                if k == 7 and s.real:
                    normalise(s, 0)
                if k == 7 and (s - 1).real:
                    n = s - 1
                    dve.wait_ge(M["rstd2_done"], (n + 1).n)
                    wait_for(dve, xn2_out[n.par], (n - 2).landed())
                    wait_for(dve, M["x2t_done"], (n - 1).n)
                    for b in range(2):
                        last = dve.tensor_scalar(xn2[:, n.par, b], x1[:, n.par, b], mv2[:, b, 0:1],
                                                 rstd2[:, b:b + 1], ALU.subtract, ALU.mult)
                    last.then_inc(M["xn2_done"], 1)

        run(dve, step)

    @block.tensor
    def _(pe):
        pe.wait_ge(M["consts_in"], 16 * 9)
        pe.wait_ge(M["w_split"], 2)
        pe.wait_ge(M["setup_dve"], 1)

        def split_matmul(out, lhs, rhs, first=True, last=True):
            (lh, ll), (rh, rl) = lhs, rhs
            pe.matmul(out, lh, rh, start=first, stop=False)
            pe.matmul(out, ll, rh, start=False, stop=False)
            return pe.matmul(out, lh, rl, start=False, stop=last)

        def scores(n, u):
            b, i = divmod(u, 4)
            U = n.n * UNITS + u
            if u == 0:
                for done in ("q_hi_done", "q_lo_done", "k_hi_done", "k_lo_done"):
                    pe.wait_ge(M[done], (n + 1).n)
            wait_for(pe, M["rowmax_done"], U - 1)
            rows = slice(32 * i, 32 * i + 32)
            for m in range(KC):
                last = split_matmul(S[u % 2][:, m * 2 * SEQ:(m + 1) * 2 * SEQ],
                                    [q[rows, n.par, m, b] for q in (q_hi, q_lo)],
                                    [k[rows, n.par, m, b].rearrange("p e t -> p (e t)") for k in (k_hi, k_lo)])
            last.then_inc(M["scores_done"], 1)

        def transpose_unit(n, u):
            U = n.n * UNITS + u
            pe.wait_ge(M["probs_done"], U + 1)
            wait_for(pe, M["pt_copied"], U - 1)
            for j in range(4):
                last = pe.transpose(PT[u % 2][:, j * SEQ:(j + 1) * SEQ], probs[:, u % 2, j], ident[:])
            last.then_inc(M["pt_done"], 1)

        def values_unit(n, u):
            b, i = divmod(u, 4)
            U = n.n * UNITS + u
            if u == 0:
                pe.wait_ge(M["v_ready"], (n + 1).n)
            pe.wait_ge(M["pt_copied"], U + 1)
            if i == 0:
                wait_for(pe, M["ot_copied"], n.n * 2 + b)
            for j in range(4):
                head = 8 * (j // 2) + 2 * i + j % 2
                last = pe.matmul(PO[32 * j:32 * j + 32, i * SEQ:(i + 1) * SEQ], v_aug[:, n.par, b, head],
                                 probs_t[:, u % 2, j], start=True, stop=True)
            last.then_inc(M["pv_done"], 1)

        def untranspose(n, b):
            pe.wait_ge(M["ot_copied"], n.n * 2 + b + 1)
            for i in range(4):
                last = pe.transpose(F2[:, i * SEQ:(i + 1) * SEQ], out_t[:, b, i], ident[:])
            last.then_inc(M["o2_done"], 1)

        def transposes(F, src):
            for k in range(KC):
                for b in range(2):
                    last = pe.transpose(F[:, (2 * k + b) * SEQ:(2 * k + b + 1) * SEQ], src[:, b, k * P:(k + 1) * P],
                                        ident[:])
            return last

        def project(F, w, hi, lo):
            for m in range(KC):
                for k in range(KC):
                    last = split_matmul(F[:, m * 2 * SEQ:(m + 1) * 2 * SEQ],
                                        [t[:, w, k, m * P:(m + 1) * P] for t in (w_hi, w_lo)],
                                        [t[:, k].rearrange("p b t -> p (b t)") for t in (hi, lo)],
                                        k == 0, k == KC - 1)
            return last

        def apply(F, w, hi, lo):
            for b in range(2):
                for k in range(KC):
                    last = split_matmul(F[:, b * DIM:(b + 1) * DIM], [t[:, k, b] for t in (hi, lo)],
                                        [t[:, w, k] for t in (w_hi, w_lo)], k == 0, k == KC - 1)
            return last

        def step(s):
            for k in range(UNITS):
                if s.real:
                    scores(s, k)
                n, u = (s, k - 2) if k >= 2 else (s - 1, k + UNITS - 2)
                if n.real:
                    transpose_unit(n, u)
                n, u = (s, k - 3) if k >= 3 else (s - 1, k + UNITS - 3)
                if n.real:
                    values_unit(n, u)
                n = s + 1
                if k == 0 and n.real:
                    pe.wait_ge(M["xn_done"], (n + 1).n)
                    wait_for(pe, M["v_ready"], n.n)
                    wait_for(pe, M["x1_done"], (n - 2).n)
                    transposes(F0, xn).then_inc(M["tx_done"], 1)
                    pe.wait_ge(c_in[n.par], n.landed())
                    wait_for(pe, M["k_scaled"], n.n)
                    wait_for(pe, M["at_lo_done"], (n - 2).n)
                    transposes(F1, c_in_sb[:, n.par]).then_inc(M["tc_done"], 1)
                if k == 0 and (s - 2).real:
                    n = s - 2
                    pe.wait_ge(M["xn2_done"], (n + 1).n)
                    pe.wait_ge(M["att_done"], (s - 1).n * 2 + 1 if (s - 1).real else 2 * PAIRS)
                    transposes(F2, xn2[:, n.par]).then_inc(M["x2t_done"], 1)
                if k == 1 and (s - 2).real:
                    n = s - 2
                    pe.wait_ge(M["x2t_copied"], (n + 1).n)
                    for kk in range(KC):
                        for b in range(2):
                            last = pe.matmul(F2[32 * b:32 * b + 32, 0:SEQ], wr[:, kk], x2t[:, kk, b],
                                             start=(kk == 0), stop=(kk == KC - 1))
                    last.then_inc(M["rt_done"], 1)
                n = s + 1
                if k == 2 and n.real:
                    for F, w, hi, lo, a, done in ((F0, 0, xt_hi, xt_lo, "xt", "qt_done"),
                                                  (F1, 1, ct_hi, ct_lo, "ct", "kt_done")):
                        pe.wait_ge(M[a + "_hi_done"], (n + 1).n)
                        pe.wait_ge(M[a + "_lo_done"], (n + 1).n)
                        project(F, w, hi, lo).then_inc(M[done], 1)
                if k == 2 and (s - 2).real:
                    n = s - 2
                    pe.wait_ge(M["lt_copied"], (n + 1).n)
                    pe.sem_inc(M["pe_passed"], 1)
                    pe.transpose(F2[:, 256:320], lt_sb[:], ident[0:64, 0:64]).then_inc(M["lg_done"], 1)
                if k == 3 and (s - 1).real:
                    wait_for(pe, M["logits_done"], (s - 1).n)
                    pe.wait_ge(M["att_done"], (s - 1).n * 2 + 1)
                    untranspose(s - 1, 1)
                n = s + 1
                if k == 4 and n.real:
                    pe.wait_ge(M["q_scaled"], (n + 1).n)
                    apply(F0, 2, ct_hi, ct_lo).then_inc(M["v_done"], 1)
                if k == 4 and (s - 1).real:
                    n = s - 1
                    pe.wait_ge(M["att_done"], n.n * 2 + 2)
                    if (s + 1).real:
                        pe.wait_ge(M["k_scaled"], (s + 2).n)
                    else:
                        pe.wait_ge(M["at_lo_done"], n.n)
                    transposes(F1, att).then_inc(M["at_done"], 1)
                if k == 6 and (s - 1).real:
                    n = s - 1
                    pe.wait_ge(M["at_hi_done"], (n + 1).n)
                    pe.wait_ge(M["at_lo_done"], (n + 1).n)
                    if (s + 1).real:
                        pe.wait_ge(M["v_ready"], (s + 2).n)
                    else:
                        pe.wait_ge(M["x1_done"], n.n)
                    apply(F0, 3, at_hi, at_lo).then_inc(M["wo_done"], 1)
                if k == 7 and s.real:
                    wait_for(pe, M["att_done"], s.n * 2)
                    untranspose(s, 0)

        run(pe, step)


def routing_block(nc, ctx, T, D):

    def sb(name, shape, dt=F32):
        return ctx.enter_context(nc.sbuf_tensor(name, shape, dt))

    def sem(name):
        return ctx.enter_context(nc.semaphore(name))

    NB = 32
    BANKS = SEQS // NB
    scaled = sb("scaled", [P, SEQS, EXPERTS])
    equal = sb("equal", [P, SEQS, EXPERTS])
    chosen = sb("chosen", [P, TOPK, SEQS, EXPERTS], BF16)
    row = sb("row", [P, 3, SEQS])
    prob = sb("prob", [P, TOPK, SEQS])
    rev_e = sb("rev_e", [P, TOPK, SEQS])
    expert = sb("expert", [P, TOPK, SEQS])
    rank = sb("rank", [P, TOPK, SEQS])
    gone = sb("gone", [P, TOPK, SEQS])
    kept = sb("kept", [P, TOPK, SEQS])
    rev = sb("rev_sb", [P, EXPERTS])
    before_f = sb("before_f", [P, P])
    before = sb("before_b", [P, P], BF16)
    ones = sb("ones_b", [P, P], BF16)
    w_in = sb("w_in", [P, T["chunks"], 1024])
    ranks = [ctx.enter_context(nc.psum_tensor(f"ranks{i}", [P, 512], F32)) for i in range(TOPK * BANKS)]
    logits, gates = T["logits"], T["gates"]
    dispatch_slot, collect_slot, weight = T["dispatch_slot"], T["collect_slot"], T["weight"]
    CH = T["chunks"]
    w_hi, w_lo = [T[w][:].rearrange("p (c n) -> p c n", c=CH) for w in ("we_hi", "we_lo")]

    consts2_in, w_landed = sem("consts2_in"), sem("w_landed")
    heads_done, rests_pool, rests_dve = sem("heads_done"), sem("rests_pool"), sem("rests_dve")
    step_done, exp_done, tables_done, ranks_done = sem("step_done"), sem("exp_done"), sem("tables_done"), sem("ranks_done")
    block = ctx.enter_context(nc.Block())

    def per_seq(a):
        return a.rearrange("p (b o) -> p b o", o=1).broadcast_to([P, SEQS, EXPERTS])

    @block.sync
    def _(sp):
        sp.dma_start(rev[:], D["rev"]).then_inc(consts2_in, 16)
        sp.dma_start(before_f[:], D["before"]).then_inc(consts2_in, 16)
        half = EXPERTS * 2 * HID
        flat = w_in[:].rearrange("p c n -> p (c n)")
        for k in range(KC):
            dst = flat[:, k * half:(k + 1) * half].rearrange("p (e f n) -> p e f n", e=EXPERTS, f=2)
            for f, name in enumerate(("w_gate", "w_fc")):
                sp.dma_start(dst[:, :, f], D[name][:, k * P:(k + 1) * P].rearrange("e c n -> c e n")) \
                    .then_inc(w_landed, 16)
        sp.dma_start(flat[:, KC * half:].rearrange("p (e n) -> p e n", e=EXPERTS),
                     D["w_proj"].rearrange("e h c -> h e c")).then_inc(w_landed, 16)
        sp.dma_start(T["iota"][:], D["iota_c"]).then_inc(consts2_in, 16)
        sp.dma_start(T["ident2"][:], D["ident"]).then_inc(consts2_in, 16)

    @block.scalar
    def _(act):
        act.wait_ge(step_done, 2)
        act.activation(scaled[:].rearrange("p b e -> p (b e)"), scaled[:].rearrange("p b e -> p (b e)"), ACT.Exp) \
            .then_inc(exp_done, 1)
        act.wait_ge(w_landed, 16 * (2 * KC + 1))
        for c in range(CH):
            act.activation(w_hi[:, c], w_in[:, c], ACT.Copy).then_inc(heads_done, 1)

    @block.gpsimd
    def _(pool):
        for c in range(CH // 2):
            pool.wait_ge(heads_done, c + 1)
            pool.tensor_tensor(w_lo[:, c], w_in[:, c], w_hi[:, c].bitcast(F32), ALU.subtract).then_inc(rests_pool, 1)
        pool.wait_ge(rests_pool, CH // 2)
        pool.wait_ge(consts2_in, 64)

    @block.tensor
    def _(pe):
        pe.wait_ge(tables_done, 2)
        pe.wait_ge(step_done, 10)
        for c in range(BANKS):
            one = chosen[:, 0, c * NB:(c + 1) * NB].rearrange("p b e -> p (b e)")
            pe.matmul(ranks[c][:, 0:NB * EXPERTS], before[:], one, start=True, stop=True)
            pe.matmul(ranks[BANKS + c][:, 0:NB * EXPERTS], ones[:], one, start=True, stop=False)
        pe.wait_ge(step_done, 16)
        for c in range(BANKS):
            two = chosen[:, 1, c * NB:(c + 1) * NB].rearrange("p b e -> p (b e)")
            last = pe.matmul(ranks[BANKS + c][:, 0:NB * EXPERTS], before[:], two, start=False, stop=True)
        last.then_inc(ranks_done, 1)

    @block.vector
    def _(dve):
        count = [0]

        def then(instruction):
            count[0] += 1
            instruction.then_inc(step_done, 1)
            dve.wait_ge(step_done, count[0])

        dve.memset(ones[:], 1.0).then_inc(tables_done, 1)
        dve.wait_ge(consts2_in, 64)
        dve.tensor_copy(before[:], before_f[:]).then_inc(tables_done, 1)
        then(dve.tensor_reduce(row[:, 0], logits[:], AX_X, ALU.max))
        then(dve.tensor_tensor(scaled[:], logits[:], per_seq(row[:, 0]), ALU.subtract))
        dve.wait_ge(exp_done, 1)
        then(dve.tensor_reduce(row[:, 1], scaled[:], AX_X, ALU.add))
        then(dve.reciprocal(row[:, 2], row[:, 1]))
        then(dve.tensor_tensor(scaled[:], scaled[:], per_seq(row[:, 2]), ALU.mult))
        all_rev = rev[:].rearrange("p (o e) -> p o e", o=1).broadcast_to([P, SEQS, EXPERTS])
        for k in range(TOPK):
            then(dve.tensor_reduce(prob[:, k], scaled[:], AX_X, ALU.max))
            then(dve.tensor_tensor(equal[:], scaled[:], per_seq(prob[:, k]), ALU.is_equal))
            then(dve.tensor_tensor(equal[:], equal[:], all_rev, ALU.mult))
            then(dve.tensor_reduce(rev_e[:, k], equal[:], AX_X, ALU.max))
            then(dve.tensor_tensor(chosen[:, k], all_rev, per_seq(rev_e[:, k]), ALU.is_equal))
            if k == 0:
                then(dve.scalar_tensor_tensor(out=scaled[:].rearrange("p b e -> p (b e)"),
                                              in0=chosen[:, 0].rearrange("p b e -> p (b e)"), scalar=-4.0,
                                              in1=scaled[:].rearrange("p b e -> p (b e)"),
                                              op0=ALU.mult, op1=ALU.add))
        then(dve.tensor_scalar(weight[:], prob[:], gates[:, 3:4], 0.5, ALU.mult, ALU.mult))
        dve.wait_ge(ranks_done, 1)
        for k in range(TOPK):
            for c in range(BANKS):
                last = dve.tensor_tensor(equal[:, c * NB:(c + 1) * NB],
                                         ranks[k * BANKS + c][:, 0:NB * EXPERTS].rearrange("p (b e) -> p b e", e=EXPERTS),
                                         chosen[:, k, c * NB:(c + 1) * NB], ALU.mult)
            then(last)
            then(dve.tensor_reduce(rank[:, k], equal[:], AX_X, ALU.add))
        then(dve.tensor_scalar(expert[:], rev_e[:], -1.0, float(EXPERTS), ALU.mult, ALU.add))
        then(dve.tensor_scalar(gone[:], rank[:], CAP - 0.5, GONE, ALU.is_gt, ALU.mult))
        then(dve.tensor_tensor(gone[:], gone[:], rank[:], ALU.add))
        then(dve.scalar_tensor_tensor(out=dispatch_slot[:], in0=expert[:], scalar=float(CAP), in1=gone[:],
                                      op0=ALU.mult, op1=ALU.add))
        then(dve.tensor_scalar(kept[:], rank[:], CAP - 1.0, float(EXPERTS), ALU.min, ALU.mult))
        then(dve.tensor_tensor(collect_slot[:], kept[:], expert[:], ALU.add))
        for c in range(CH // 2, CH):
            dve.wait_ge(heads_done, c + 1)
            last = dve.tensor_tensor(w_lo[:, c], w_in[:, c], w_hi[:, c].bitcast(F32), ALU.subtract)
        last.then_inc(rests_dve, 1)
        dve.wait_ge(rests_dve, 1)


class Unit:

    def __init__(self, i, c):
        self.i, self.c = i + c // 2, c % 2

    def __sub__(self, d):
        return Unit(self.i, self.c - d)

    @property
    def n(self):
        return self.i * 2 + self.c

    @property
    def group(self):
        return self.i // (GROUP // 2)

    @property
    def j(self):
        return self.i % (GROUP // 2) * 2 + self.c

    @property
    def landed(self):
        return (self.i + 1) * 16


def expert_block(nc, ctx, T, D):
    LOAD, PICK, DISPATCH, SPLIT, GATE, HIDDEN, OUTPUT, FETCH, MIX, COLLECT = -14, -12, -10, -2, 0, 2, 4, 12, 14, 16

    def sb(name, shape, dt=F32):
        return ctx.enter_context(nc.sbuf_tensor(name, shape, dt))

    def sem(name):
        return ctx.enter_context(nc.semaphore(name))

    def pb(name):
        return ctx.enter_context(nc.psum_tensor(name, [P, 512], F32))

    x_in_sb = sb("xn2_sb", [P, 2, DIM])
    x_hi = sb("x_hi", [P, 2, DIM], F32R)
    x_lo = sb("x_lo", [P, 2, DIM], F32R)
    pick1 = sb("pick1", [P, 2, SLOTS])
    pick = sb("pick", [P, 2, SLOTS], F32R)
    slots = sb("slots", [P, 2, KC, EXPERTS, GROUP, CAP])
    s_hi = sb("s_hi", [P, 2, KC, 2, P], F32R)
    s_lo = sb("s_lo", [P, 2, KC, 2, P], F32R)
    th = sb("th", [P, 2, 2, HID])
    gated = sb("gated", [P, 2, HID])
    hid = sb("hid", [P, 2, 2, HID])
    h_hi = sb("h_hi", [P, 2, 2, P], F32R)
    h_lo = sb("h_lo", [P, 2, 2, P], F32R)
    eo = sb("eo", [P, 2, 2, DIM])
    e_in = sb("e_in", [P, 2, 2, DIM])
    e_hi = sb("e_hi", [P, 2, 2, DIM], F32R)
    e_lo = sb("e_lo", [P, 2, 2, DIM], F32R)
    mix1 = sb("mix1", [P, SLOTS])
    mix2 = sb("mix2", [P, SLOTS])
    mix = sb("mix", [P, 2, SLOTS])
    m_hi = sb("m_hi", [P, 2, 2, P], F32R)
    m_lo = sb("m_lo", [P, 2, 2, P], F32R)
    xr = sb("xr", [P, 4, DIM])
    y_sb = sb("y_sb", [P, 2, DIM])
    ident, iota = T["ident2"], T["iota"]
    dispatch_slot, collect_slot, weight = T["dispatch_slot"], T["collect_slot"], T["weight"]
    half = EXPERTS * 2 * HID
    w_gu = [T[w][:, 0:KC * half].rearrange("p (k n) -> p k n", k=KC) for w in ("we_hi", "we_lo")]
    w_down = [T[w][:, KC * half:] for w in ("we_hi", "we_lo")]

    names = ("x_hi_done x_lo_done pick1_done pick_done ds_done slots_done s_hi_done s_lo_done gu_done th_done "
             "gated_done hid_done ht_done h_hi_done h_lo_done eo_done eo_copied e_hi_done e_lo_done mix12_done "
             "mix_done mt_done m_hi_done m_lo_done y_done out_done").split()
    M = {n: sem(n) for n in names}
    x_in = [sem("xn2_in0"), sem("xn2_in1")]
    e_landed = [sem("e_in0"), sem("e_in1")]
    x1_in = [sem("x1_in0"), sem("x1_in1")]
    eo_out = [sem("eo_out0"), sem("eo_out1")]
    y_out = [sem("y_out0"), sem("y_out1")]
    DS, HT, EO, MT, Y = pb("DS"), pb("HT"), pb("EOB"), pb("MT"), pb("Y")
    GU = [pb("GU0"), pb("GU1")]
    block = ctx.enter_context(nc.Block())

    def run(eng, step):
        lags = (LOAD, PICK, DISPATCH, SPLIT, GATE, HIDDEN, OUTPUT, FETCH, MIX, COLLECT)
        cuts = sorted({e + x for x in lags for e in (0, 2, SEQS)})
        for a, b in zip(cuts, cuts[1:]):
            def on(lag):
                return lag <= a and b <= SEQS + lag
            if b - a <= 2:
                for u in range(a, b):
                    step(lambda lag: Unit(0, u - lag), on)
            else:
                with eng.Fori((a - LOAD) // 2, (b - LOAD) // 2) as i:
                    for c in range(2):
                        step(lambda lag: Unit(i, c - (lag - LOAD)), on)

    def flat(a):
        return a.rearrange("p a b -> p (a b)")

    @block.sync
    def _(sp):
        def step(unit, on):
            n = unit(LOAD)
            if on(LOAD):
                wait_for(sp, M["x_lo_done"], n.n - 1)
                sp.dma_start(x_in_sb[:, n.c], D["xn2_d"][:, n.n]).then_inc(x_in[n.c], 16)
            n = unit(OUTPUT)
            if on(OUTPUT):
                sp.wait_ge(M["eo_copied"], n.n + 1)
                sp.dma_start(D["eo_d"][bass.ds(n.group * P, P), bass.ds(n.j * 2, 2)], eo[:, n.c]) \
                    .then_inc(eo_out[n.c], 16)
            n = unit(FETCH)
            if on(FETCH):
                for q in eo_out:
                    sp.wait_ge(q, (n.group + 1) * (GROUP // 2) * 16)
                wait_for(sp, M["e_lo_done"], n.n - 1)
                sp.dma_start(e_in[:, n.c], D["eo_d"][bass.ds(n.n * CAP, CAP)]
                             .rearrange("r e c -> (r e) c").rearrange("(h p) c -> p h c", h=2)).then_inc(e_landed[n.c], 16)
                wait_for(sp, M["out_done"], n.n - 3)
                sp.dma_start(xr[:, bass.ds(n.n % 4, 1)], D["x1_d"][:, bass.ds(n.n, 1)]).then_inc(x1_in[n.c], 16)
            n = unit(COLLECT)
            if on(COLLECT):
                sp.wait_ge(M["out_done"], n.n + 1)
                sp.dma_start(D["out"][bass.ds(n.n, 1)].rearrange("b t c -> t b c"), y_sb[:, n.c:n.c + 1]) \
                    .then_inc(y_out[n.c], 16)

        run(sp, step)
        for q in y_out:
            sp.wait_ge(q, 16 * (SEQS // 2))

    @block.gpsimd
    def _(pool):
        def step(unit, on):
            n = unit(PICK)
            if on(PICK):
                pool.wait_ge(M["x_hi_done"], n.n + 1)
                wait_for(pool, M["ds_done"], n.n - 1)
                pool.tensor_tensor(x_lo[:, n.c], x_in_sb[:, n.c], x_hi[:, n.c].bitcast(F32), ALU.subtract) \
                    .then_inc(M["x_lo_done"], 1)
            n = unit(MIX)
            if on(MIX):
                pool.wait_ge(M["e_hi_done"], n.n + 1)
                wait_for(pool, M["y_done"], n.n - 1)
                pool.tensor_tensor(flat(e_lo[:, n.c]), flat(e_in[:, n.c]), flat(e_hi[:, n.c]).bitcast(F32),
                                   ALU.subtract).then_inc(M["e_lo_done"], 1)
            n = unit(SPLIT)
            if on(SPLIT):
                pool.wait_ge(M["s_hi_done"], n.n + 1)
                wait_for(pool, M["gu_done"], n.n - 1)
                src = slots[:, bass.ds(n.group % 2, 1), :, bass.ds(n.j * 2, 2)].rearrange("p o k e b s -> p (o k) e (b s)")
                pool.tensor_tensor(s_lo[:, n.c], src, s_hi[:, n.c].bitcast(F32), ALU.subtract) \
                    .then_inc(M["s_lo_done"], 1)

        run(pool, step)

    @block.scalar
    def _(act):
        def step(unit, on):
            n = unit(DISPATCH)
            if on(DISPATCH):
                act.wait_ge(M["ds_done"], n.n + 1)
                if on(SPLIT):
                    wait_for(act, M["s_lo_done"], n.n - GROUP)
                dst = slots[:, bass.ds(n.group % 2, 1), :, :, bass.ds(n.j, 1)] \
                    .rearrange("p o k e b s -> p (o k) e (b s)")
                act.activation(dst, DS[:].rearrange("p (k e s) -> p k e s", k=KC, s=CAP), ACT.Copy) \
                    .then_inc(M["slots_done"], 1)
            n = unit(PICK)
            if on(PICK):
                act.wait_ge(x_in[n.c], n.landed)
                wait_for(act, M["ds_done"], n.n - 1)
                act.activation(x_hi[:, n.c], x_in_sb[:, n.c], ACT.Copy).then_inc(M["x_hi_done"], 1)
            n = unit(MIX)
            if on(MIX):
                act.wait_ge(M["mt_done"], n.n + 1)
                wait_for(act, M["y_done"], n.n - 1)
                act.activation(flat(m_hi[:, n.c]), MT[:, 0:2 * P], ACT.Copy).then_inc(M["m_hi_done"], 1)
                act.wait_ge(e_landed[n.c], n.landed)
                act.activation(flat(e_hi[:, n.c]), flat(e_in[:, n.c]), ACT.Copy).then_inc(M["e_hi_done"], 1)
            n = unit(OUTPUT)
            if on(OUTPUT):
                act.wait_ge(M["eo_done"], n.n + 1)
                wait_for(act, eo_out[n.c], (n - 2).landed)
                act.activation(flat(eo[:, n.c]), EO[:], ACT.Copy).then_inc(M["eo_copied"], 1)
            n = unit(HIDDEN)
            if on(HIDDEN):
                act.wait_ge(M["ht_done"], n.n + 1)
                wait_for(act, M["eo_done"], n.n - 1)
                act.activation(flat(h_hi[:, n.c]), HT[:, 0:2 * P], ACT.Copy).then_inc(M["h_hi_done"], 1)
            n = unit(SPLIT)
            if on(SPLIT):
                act.wait_ge(M["slots_done"], (n.group + 1) * GROUP)
                wait_for(act, M["gu_done"], n.n - 1)
                src = slots[:, bass.ds(n.group % 2, 1), :, bass.ds(n.j * 2, 2)].rearrange("p o k e b s -> p (o k) e (b s)")
                act.activation(s_hi[:, n.c], src, ACT.Copy).then_inc(M["s_hi_done"], 1)
            n = unit(GATE)
            if on(GATE):
                act.wait_ge(M["gu_done"], n.n + 1)
                wait_for(act, M["gated_done"], n.n - 1)
                act.activation(th[:, n.c], GU[n.c][:].rearrange("p (e f n) -> p e f n", e=2, f=2)[:, :, 0],
                               ACT.Tanh, scale=0.5).then_inc(M["th_done"], 1)

        run(act, step)

    @block.vector
    def _(dve):
        def step(unit, on):
            n = unit(PICK)
            if on(PICK):
                wait_for(dve, M["pick_done"], n.n - 1)
                dve.tensor_scalar(pick1[:, n.c], iota[:], dispatch_slot[:, 0, bass.ds(n.n, 1)], None, ALU.is_equal) \
                    .then_inc(M["pick1_done"], 1)
            n = unit(MIX)
            if on(MIX):
                dve.wait_ge(M["m_hi_done"], n.n + 1)
                wait_for(dve, M["y_done"], n.n - 1)
                dve.tensor_tensor(flat(m_lo[:, n.c]), MT[:, 0:2 * P], flat(m_hi[:, n.c]).bitcast(F32), ALU.subtract) \
                    .then_inc(M["m_lo_done"], 1)
            n = unit(PICK)
            if on(PICK):
                dve.wait_ge(M["pick1_done"], n.n + 1)
                wait_for(dve, M["ds_done"], n.n - 1)
                dve.scalar_tensor_tensor(out=pick[:, n.c], in0=iota[:], scalar=dispatch_slot[:, 1, bass.ds(n.n, 1)],
                                         in1=pick1[:, n.c], op0=ALU.is_equal, op1=ALU.add) \
                    .then_inc(M["pick_done"], 1)
            n = unit(FETCH)
            if on(FETCH):
                wait_for(dve, M["mix_done"], n.n)
                for dst, k in ((mix1, 0), (mix2, 1)):
                    last = dve.tensor_scalar(dst[:], iota[:], collect_slot[:, k, bass.ds(n.n, 1)],
                                             weight[:, k, bass.ds(n.n, 1)], ALU.is_equal, ALU.mult)
                last.then_inc(M["mix12_done"], 1)
            n = unit(COLLECT)
            if on(COLLECT):
                dve.wait_ge(M["y_done"], n.n + 1)
                dve.wait_ge(x1_in[n.c], n.landed)
                wait_for(dve, y_out[n.c], (n - 2).landed)
                dve.tensor_tensor(y_sb[:, n.c:n.c + 1], Y[:, 0:DIM].rearrange("p (o c) -> p o c", o=1),
                                  xr[:, bass.ds(n.n % 4, 1)], ALU.add).then_inc(M["out_done"], 1)
            n = unit(FETCH)
            if on(FETCH):
                dve.wait_ge(M["mix12_done"], n.n + 1)
                wait_for(dve, M["mt_done"], n.n - 1)
                dve.tensor_tensor(mix[:, n.c], mix1[:], mix2[:], ALU.add).then_inc(M["mix_done"], 1)
            n = unit(HIDDEN)
            if on(HIDDEN):
                dve.wait_ge(M["h_hi_done"], n.n + 1)
                wait_for(dve, M["eo_done"], n.n - 1)
                dve.tensor_tensor(flat(h_lo[:, n.c]), HT[:, 0:2 * P], flat(h_hi[:, n.c]).bitcast(F32), ALU.subtract) \
                    .then_inc(M["h_lo_done"], 1)
            n = unit(GATE)
            if on(GATE):
                gu = GU[n.c][:].rearrange("p (e f n) -> p e f n", e=2, f=2)
                dve.wait_ge(M["th_done"], n.n + 1)
                wait_for(dve, M["hid_done"], n.n)
                dve.scalar_tensor_tensor(out=gated[:], in0=th[:, n.c], scalar=1.0, in1=gu[:, :, 0],
                                         op0=ALU.add, op1=ALU.mult).then_inc(M["gated_done"], 1)
                dve.wait_ge(M["gated_done"], n.n + 1)
                wait_for(dve, M["ht_done"], n.n - 1)
                dve.tensor_tensor(hid[:, n.c], gated[:], gu[:, :, 1], ALU.mult).then_inc(M["hid_done"], 1)

        run(dve, step)

    @block.tensor
    def _(pe):
        def split_matmul(out, lhs, rhs, first=True, last=True):
            (lh, ll), (rh, rl) = lhs, rhs
            pe.matmul(out, lh, rh, start=first, stop=False)
            pe.matmul(out, ll, rh, start=False, stop=False)
            return pe.matmul(out, lh, rl, start=False, stop=last)

        def step(unit, on):
            n = unit(DISPATCH)
            if on(DISPATCH):
                pe.wait_ge(M["pick_done"], n.n + 1)
                pe.wait_ge(M["x_hi_done"], n.n + 1)
                pe.wait_ge(M["x_lo_done"], n.n + 1)
                wait_for(pe, M["slots_done"], n.n)
                for k in range(KC):
                    out = DS[:, k * SLOTS:(k + 1) * SLOTS]
                    pe.matmul(out, x_hi[:, n.c, k * P:(k + 1) * P], pick[:, n.c], start=True, stop=False)
                    last = pe.matmul(out, x_lo[:, n.c, k * P:(k + 1) * P], pick[:, n.c], start=False, stop=True)
                last.then_inc(M["ds_done"], 1)
            n = unit(MIX)
            if on(MIX):
                pe.wait_ge(M["mix_done"], n.n + 1)
                wait_for(pe, M["m_lo_done"], n.n)
                for h in range(2):
                    last = pe.transpose(MT[:, h * P:(h + 1) * P], mix[:, n.c, h * P:(h + 1) * P], ident[:])
                last.then_inc(M["mt_done"], 1)

            n = unit(COLLECT)
            if on(COLLECT):
                for done in ("e_hi_done", "e_lo_done", "m_hi_done", "m_lo_done"):
                    pe.wait_ge(M[done], n.n + 1)
                wait_for(pe, M["out_done"], n.n)
                for h in range(2):
                    last = split_matmul(Y[:, 0:DIM], [m[:, n.c, h] for m in (m_hi, m_lo)],
                                        [e[:, n.c, h] for e in (e_hi, e_lo)], h == 0, h == 1)
                last.then_inc(M["y_done"], 1)
            n = unit(OUTPUT)
            if on(OUTPUT):
                for done in ("h_hi_done", "h_lo_done"):
                    pe.wait_ge(M[done], n.n + 1)
                wait_for(pe, M["eo_copied"], n.n)
                for e in range(2):
                    last = split_matmul(EO[:, e * DIM:(e + 1) * DIM], [h[:, n.c, e] for h in (h_hi, h_lo)],
                                        [w[:, bass.ds(n.j * (2 * DIM) + e * DIM, DIM)] for w in w_down])
                last.then_inc(M["eo_done"], 1)
            n = unit(HIDDEN)
            if on(HIDDEN):
                pe.wait_ge(M["hid_done"], n.n + 1)
                wait_for(pe, M["h_lo_done"], n.n)
                for e in range(2):
                    last = pe.transpose(HT[:, e * P:(e + 1) * P], hid[:, n.c, e], ident[:])
                last.then_inc(M["ht_done"], 1)
            n = unit(GATE)
            if on(GATE):
                for done in ("s_hi_done", "s_lo_done"):
                    pe.wait_ge(M[done], n.n + 1)
                wait_for(pe, M["hid_done"], n.n - 1)
                for e in range(2):
                    for k in range(KC):
                        last = split_matmul(GU[n.c][:, e * 2 * HID:(e + 1) * 2 * HID],
                                            [t[:, n.c, k, e] for t in (s_hi, s_lo)],
                                            [w[:, k, bass.ds(n.j * (4 * HID) + e * 2 * HID, 2 * HID)] for w in w_gu],
                                            k == 0, k == KC - 1)
                last.then_inc(M["gu_done"], 1)

        run(pe, step)


def flamingo_kernel(nc, D):
    with ExitStack() as outer:
        def sb(name, shape, dt=F32):
            return outer.enter_context(nc.sbuf_tensor(name, shape, dt))

        D["x1_d"] = nc.dram_tensor("x1_d", [P, SEQS, DIM], F32).ap()
        D["xn2_d"] = nc.dram_tensor("xn2_d", [P, SEQS, DIM], F32).ap()
        D["eo_d"] = nc.dram_tensor("eo_d", [SEQS * CAP, EXPERTS, DIM], F32).ap()
        T = {"gates": sb("gates", [P, 4]), "logits": sb("logits", [P, SEQS, EXPERTS])}
        with ExitStack() as ctx:
            attention_block(nc, ctx, T, D)
        for name in ("dispatch_slot", "collect_slot", "weight"):
            T[name] = sb(name, [P, TOPK, SEQS])
        T["iota"], T["ident2"] = sb("iota_sb", [P, SLOTS]), sb("ident2", [P, P])
        size = KC * EXPERTS * 2 * HID + EXPERTS * DIM
        T["chunks"] = size // 1024
        T["we_hi"], T["we_lo"] = sb("we_hi", [P, size], F32R), sb("we_lo", [P, size], F32R)
        with ExitStack() as ctx:
            routing_block(nc, ctx, T, D)
        with ExitStack() as ctx:
            expert_block(nc, ctx, T, D)


def kernel(**inputs):
    import concourse.bacc as bacc
    from concourse.bass_utils import run_bass_kernel_spmd

    a = {k: np.ascontiguousarray(v) for k, v in inputs.items()}
    wo = np.ascontiguousarray(
        a["L0_xattn_wo_w"].T.reshape(KC, 4, 2, DK, DIM).transpose(1, 0, 2, 3, 4).reshape(DIM, DIM))
    inv_freq = (1.0 / 10000.0 ** (np.arange(P, dtype=np.float32) / np.float32(P))).astype(np.float32)
    angle = inv_freq[:, None] * np.arange(SEQ, dtype=np.float32)[None, :]
    at = np.arange(P)
    arrays = {
        "x": a["x"], "ctx": a["ctx_1024"], "g_xattn": a["g_xattn"], "g_ffn": a["g_ffn"],
        "wq": np.ascontiguousarray(a["L0_xattn_wq"].T), "wk": np.ascontiguousarray(a["L0_xattn_wk"].T),
        "wv": np.ascontiguousarray(a["L0_xattn_wv"].T), "wo": wo, "wo_b": a["L0_xattn_wo_b"],
        "w_router": a["L0_ffn_w_router"], "w_fc": a["L0_ffn_w_fc"], "w_gate": a["L0_ffn_w_gate"],
        "w_proj": a["L0_ffn_w_proj"],
        "cos": np.cos(angle).astype(np.float32), "sin": np.sin(angle).astype(np.float32),
        "band": np.where(np.abs(at[:, None] - at[None, :]) <= WINDOW, 0.0, FAR).astype(np.float32),
        "kmask": np.stack([np.where(at // DK % 2 == e, -float(DK) ** 0.5, 0.0) for e in range(2)], 1).astype(np.float32),
        "ident": np.eye(P, dtype=np.float32),
        "rev": np.broadcast_to(EXPERTS - np.arange(EXPERTS, dtype=np.float32), (P, EXPERTS)).copy(),
        "before": (at[:, None] < at[None, :]).astype(np.float32),
        "iota_c": np.broadcast_to(np.arange(SLOTS, dtype=np.float32), (P, SLOTS)).copy(),
    }
    nc = bacc.Bacc("TRN2", target_bir_lowering=False, num_devices=1)
    D = {n: nc.dram_tensor(n, v.shape, F32, kind="ExternalInput").ap() for n, v in arrays.items()}
    D["out"] = nc.dram_tensor("out", [SEQS, SEQ, DIM], F32, kind="ExternalOutput").ap()
    flamingo_kernel(nc, D)
    r = run_bass_kernel_spmd(nc, [arrays], core_ids=[0])
    return r.results[0]["out"]
```

```python
from contextlib import ExitStack

import numpy as np

import concourse.bass as bass
from concourse import mybir

F32 = mybir.dt.float32
F32R = mybir.dt.float32r
BF16 = mybir.dt.bfloat16
ALU = mybir.AluOpType
ACT = mybir.ActivationFunctionType
AX_X = mybir.AxisListType.X

P = 128
SEQS, SEQ, DIM = 128, 128, 256
HEADS = 16
DK = DIM // HEADS
WINDOW = 64
KC = DIM // P
PAIRS = SEQS // 2
UNITS = 8
EXPERTS, TOPK, HID = 16, 2, 128
CAP = TOPK * SEQ // EXPERTS
SLOTS = EXPERTS * CAP
GROUP = P // CAP
GROUPS = SEQS // GROUP
EPS = 1e-5
FAR = float(2.0 ** 100)
EARLY = SEQS - 4
GONE = 1000.0


def wait_for(eng, sem, value):
    if isinstance(value, int) and value <= 0:
        return
    eng.wait_ge(sem, value)


class Pair:

    def __init__(self, i, c):
        self.i, self.c = i, c

    def __add__(self, d):
        return Pair(self.i, self.c + d)

    def __sub__(self, d):
        return Pair(self.i, self.c - d)

    @property
    def n(self):
        return self.i * 2 + self.c

    @property
    def par(self):
        return self.c % 2

    @property
    def half(self):
        return self.i + self.c // 2

    @property
    def beyond(self):
        return self.i * 2 + self.c - PAIRS if isinstance(self.i, int) else -1

    @property
    def real(self):
        return not isinstance(self.i, int) or 0 <= self.i * 2 + self.c < PAIRS

    def landed(self):
        return (self.half + 1) * 16


def attention_block(nc, ctx, T, D):

    def sb(name, shape, dt=F32):
        return ctx.enter_context(nc.sbuf_tensor(name, shape, dt))

    def pb(name):
        return ctx.enter_context(nc.psum_tensor(name, [P, 512], F32))

    def sem(name):
        return ctx.enter_context(nc.semaphore(name))

    x_in_sb = sb("x_in_sb", [P, 2, 2, DIM])
    c_in_sb = sb("c_in_sb", [P, 2, 2, DIM])
    xr_sb = sb("xr_sb", [P, 2, 2, DIM])
    xb = sb("xb", [P, 2, DIM])
    stage = sb("stage", [P, 4, KC, DIM])
    w_hi = sb("w_hi", [P, 4, KC, DIM], F32R)
    w_lo = sb("w_lo", [P, 4, KC, DIM], F32R)
    wr = sb("wr", [P, KC, 32])
    tb = sb("tb", [P, DIM])
    cos = sb("cos_sb", [P, SEQ])
    sin = sb("sin_sb", [P, SEQ])
    band = sb("band_sb", [P, SEQ])
    kmask = sb("kmask_sb", [P, 2])
    ident = sb("ident_sb", [P, P])
    stats = sb("stats", [P, 2, 6])
    stats2 = sb("stats2", [P, 2, 6])
    mv = sb("mv", [P, 2, 2])
    mv2 = sb("mv2", [P, 2, 2])
    ve = sb("ve", [P, 2])
    ve2 = sb("ve2", [P, 2])
    rstd = sb("rstd", [P, 2])
    rstd2 = sb("rstd2", [P, 2])
    mhalf = sb("mhalf", [P, 2])
    xn = sb("xn", [P, 2, DIM])
    xt_hi = sb("xt_hi", [P, KC, 2, SEQ], F32R)
    xt_lo = sb("xt_lo", [P, KC, 2, SEQ], F32R)
    ct_hi = sb("ct_hi", [P, KC, 2, SEQ], F32R)
    ct_lo = sb("ct_lo", [P, KC, 2, SEQ], F32R)
    q_cos = sb("q_cos", [P, KC, 2 * SEQ])
    q_sin = sb("q_sin", [P, KC, 2 * SEQ])
    k_cos = sb("k_cos", [P, KC, 2 * SEQ])
    k_sin = sb("k_sin", [P, KC, 2 * SEQ])
    q_rot = sb("q_rot", [P, KC, 2 * SEQ])
    k_rot = sb("k_rot", [P, KC, 2 * SEQ])
    q_hi = sb("q_hi", [P, 2, KC, 2, SEQ], F32R)
    q_lo = sb("q_lo", [P, 2, KC, 2, SEQ], F32R)
    k_hi = sb("k_hi", [P, 2, KC, 2, 2, SEQ], F32R)
    k_lo = sb("k_lo", [P, 2, KC, 2, 2, SEQ], F32R)
    v_aug = sb("v_aug", [P, 2, 2, HEADS, 32])
    neg_s = sb("neg_s", [P, 2, 4, SEQ])
    neg_max = sb("neg_max", [P, 2, 4])
    probs = sb("probs", [P, 2, 4, SEQ])
    probs_t = sb("probs_t", [P, 2, 4, SEQ])
    out_t = sb("out_t", [P, 2, 4, SEQ])
    rden = sb("rden", [P, 2, HEADS])
    att = sb("att", [P, 2, DIM])
    at_hi = sb("at_hi", [P, KC, 2, SEQ], F32R)
    at_lo = sb("at_lo", [P, KC, 2, SEQ], F32R)
    x1 = sb("x1", [P, 2, 2, DIM])
    xn2 = sb("xn2", [P, 2, 2, DIM])
    x2t = sb("x2t", [P, KC, 2, SEQ])
    lt_sb = sb("lt_sb", [64, SEQ])
    gates = T["gates"]
    logits = T["logits"]

    S = [pb("S0"), pb("S1")]
    PT = [pb("PT0"), pb("PT1")]
    PO = pb("PO")
    F0, F1, F2 = pb("F0"), pb("F1"), pb("F2")

    names = ("consts_in wproj_in w_split gate_tanh setup_dve setup_pool tb_done "
             "ln_stats ln_aggr rstd_done ve_done xn_done xb_done "
             "tx_done tc_done xt_hi_done xt_lo_done ct_hi_done ct_lo_done qt_done kt_done v_done "
             "q_scaled k_scaled q_rotated k_rotated q_hi_done q_lo_done k_hi_done k_lo_done v_ready "
             "scores_done rowmax_done probs_done pt_done pt_copied pv_done ot_copied o2_done rden_done att_done "
             "at_done at_hi_done at_lo_done wo_done x1_done ln2_stats ln2_aggr ve2_done rstd2_done xn2_done "
             "x2t_done x2t_copied rt_done lt_copied lg_done logits_done "
             "dve_passed pe_passed pool_passed soft_step soft_exp").split()
    M = {n: sem(n) for n in names}
    x_in = [sem("x_in0"), sem("x_in1")]
    c_in = [sem("c_in0"), sem("c_in1")]
    xr_in = [sem("xr_in0"), sem("xr_in1")]
    x1_out = [sem("x1_out0"), sem("x1_out1")]
    xn2_out = [sem("xn2_out0"), sem("xn2_out1")]

    def run(eng, step):
        for c in range(-3, 2):
            step(Pair(0, c))
        with eng.Fori(1, PAIRS // 2 - 2) as i:
            step(Pair(i, 0))
            step(Pair(i, 1))
        for c in range(PAIRS - 4, PAIRS + 2):
            step(Pair(0, c))

    block = ctx.enter_context(nc.Block())

    @block.sync
    def _(sp):
        for k, name in enumerate(("wq", "wk", "wv", "wo")):
            sp.dma_start(stage[:, k], D[name].rearrange("(k p) e -> p k e", p=P)).then_inc(M["wproj_in"], 16)
        for dst, name in ((cos, "cos"), (sin, "sin"), (band, "band"), (kmask, "kmask"), (ident, "ident")):
            sp.dma_start(dst[:], D[name]).then_inc(M["consts_in"], 16)
        sp.dma_start(wr[:, :, 0:EXPERTS], D["w_router"].rearrange("(k p) e -> p k e", p=P)).then_inc(M["consts_in"], 16)
        sp.dma_start(tb[:], D["wo_b"].partition_broadcast(P)).then_inc(M["consts_in"], 16)
        sp.dma_start(gates[:, 0:1], D["g_xattn"].partition_broadcast(P)).then_inc(M["consts_in"], 16)
        sp.dma_start(gates[:, 1:2], D["g_ffn"].partition_broadcast(P)).then_inc(M["consts_in"], 16)

        half = EXPERTS * 2 * HID
        flat = T["w_in"][:]
        expert_weights = [(flat[:, k * half:(k + 1) * half].rearrange("p (e f n) -> p e f n", e=EXPERTS, f=2)[:, :, f],
                           D[name][:, k * P:(k + 1) * P].rearrange("e c n -> c e n"))
                          for k in range(KC) for f, name in enumerate(("w_gate", "w_fc"))]
        expert_weights.append((flat[:, KC * half:].rearrange("p (e n) -> p e n", e=EXPERTS),
                               D["w_proj"].rearrange("e h c -> h e c")))

        def step(s):
            n = s + 3
            if n.real:
                wait_for(sp, M["xn_done"], (n - 1).n)
                sp.dma_start(x_in_sb[:, n.par], D["x"][bass.ds(n.n * 2, 2)].rearrange("b t c -> t b c")) \
                    .then_inc(x_in[n.par], 16)
            n = s + 2
            if n.real:
                wait_for(sp, M["tc_done"], (n - 1).n)
                sp.dma_start(c_in_sb[:, n.par], D["ctx"][bass.ds(n.n * 2, 2)].rearrange("b t c -> t b c")) \
                    .then_inc(c_in[n.par], 16)
            n = s
            if n.real:
                wait_for(sp, M["xb_done"], (n - 1).n)
                sp.dma_start(xr_sb[:, n.par], D["x"][bass.ds(n.n * 2, 2)].rearrange("b t c -> t b c")) \
                    .then_inc(xr_in[n.par], 16)
            if s.beyond == -4:
                sp.dma_start(T["rev"][:], D["rev"]).then_inc(T["tables_in"], 16)
                sp.dma_start(T["before_f"][:], D["before"]).then_inc(T["tables_in"], 16)
            if isinstance(s.i, int) and 0 <= s.c - (PAIRS - 4) < len(expert_weights):
                dst, src = expert_weights[s.c - (PAIRS - 4)]
                sp.dma_start(dst, src).then_inc(T["w_landed"], 16)
            n = s - 2
            if n.real:
                sp.wait_ge(M["x1_done"], (n + 1).n)
                sp.dma_start(D["x1_d"][:, bass.ds(n.n * 2, 2)], x1[:, n.par]).then_inc(x1_out[n.par], 16)
                sp.wait_ge(M["xn2_done"], (n + 1).n)
                sp.dma_start(D["xn2_d"][:, bass.ds(n.n * 2, 2)], xn2[:, n.par]).then_inc(xn2_out[n.par], 16)

        run(sp, step)
        for q in x1_out + xn2_out:
            sp.wait_ge(q, 16 * (PAIRS // 2))

    @block.gpsimd
    def _(pool):
        pool.memset(mhalf[:], -0.5).then_inc(M["setup_pool"], 1)
        pool.memset(v_aug[:, :, :, :, DK:32], 1.0).then_inc(M["setup_pool"], 1)
        pool.wait_ge(M["setup_pool"], 2)
        pool.wait_ge(M["tb_done"], 1)

        def residual(n):
            pool.wait_ge(xr_in[n.par], n.landed())
            wait_for(pool, M["x1_done"], n.n)
            for b in range(2):
                last = pool.tensor_tensor(xb[:, b], xr_sb[:, n.par, b], tb[:], ALU.add)
            last.then_inc(M["xb_done"], 1)

        def scale_of_norm(n):
            pool.wait_ge(M["ve_done"], (n + 1).n)
            wait_for(pool, M["xn_done"], n.n)
            pool.tensor_tensor(rstd[:], ve[:], mhalf[:], ALU.pow).then_inc(M["rstd_done"], 1)

        def normed(n):
            pool.wait_ge(M["rstd_done"], (n + 1).n)
            wait_for(pool, M["tx_done"], n.n)
            pool.sem_inc(M["pool_passed"], 1)
            for b in range(2):
                last = pool.tensor_scalar(xn[:, b], x_in_sb[:, n.par, b], mv[:, b, 0:1], rstd[:, b:b + 1],
                                          ALU.subtract, ALU.mult)
            last.then_inc(M["xn_done"], 1)

        def rotate(n, a):
            qc, qs, rot = {"q": (q_cos, q_sin, q_rot), "k": (k_cos, k_sin, k_rot)}[a]
            pool.wait_ge(M[a + "_scaled"], (n + 1).n)
            for done in (a + "_hi_done", a + "_lo_done"):
                wait_for(pool, M[done], n.n)
            pool.tensor_tensor(rot[:, 0], qc[:, 0], qs[:, 1], ALU.subtract)
            pool.tensor_tensor(rot[:, 1], qc[:, 1], qs[:, 0], ALU.add).then_inc(M[a + "_rotated"], 1)

        def query_rest(n):
            pool.wait_ge(M["q_hi_done"], (n + 1).n)
            wait_for(pool, M["scores_done"], (n - 1).n * UNITS)
            pool.wait_ge(M["q_rotated"], (n + 1).n)
            pool.tensor_tensor(q_lo[:, n.par].rearrange("p k b t -> p (k b t)"),
                               q_rot[:].rearrange("p k t -> p (k t)"),
                               q_hi[:, n.par].rearrange("p k b t -> p (k b t)").bitcast(F32), ALU.subtract) \
                .then_inc(M["q_lo_done"], 1)

        def scale_of_norm2(n):
            pool.wait_ge(M["ve2_done"], (n + 1).n)
            wait_for(pool, M["xn2_done"], n.n)
            pool.tensor_tensor(rstd2[:], ve2[:], mhalf[:], ALU.pow).then_inc(M["rstd2_done"], 1)

        def step(s):
            if (s - 1).real:
                residual(s - 1)
            if (s + 2).real:
                scale_of_norm(s + 2)
            if (s + 1).real:
                rotate(s + 1, "q")
            if (s + 2).real:
                normed(s + 2)
            if (s + 1).real:
                rotate(s + 1, "k")
            if (s + 1).real:
                query_rest(s + 1)
            if (s - 1).real:
                scale_of_norm2(s - 1)

        run(pool, step)

    @block.scalar
    def _(act):
        act.wait_ge(M["consts_in"], 16 * 9)
        act.activation(gates[:, 2:4], gates[:, 0:2], ACT.Tanh).then_inc(M["gate_tanh"], 1)
        act.wait_ge(M["wproj_in"], 64)
        act.activation(w_hi[:].rearrange("p a k e -> p (a k e)"), stage[:].rearrange("p a k e -> p (a k e)"), ACT.Copy) \
            .then_inc(M["w_split"], 1)

        def exp_unit(n, u):
            U = n.n * UNITS + u
            act.wait_ge(M["rowmax_done"], U + 1)
            wait_for(act, M["pt_done"], U - 1)
            for j in range(4):
                last = act.activation(probs[:, u % 2, j], neg_s[:, u % 2, j], ACT.Exp,
                                      bias=neg_max[:, u % 2, j:j + 1], scale=-1.0)
            last.then_inc(M["probs_done"], 1)

        def copy_unit(n, u):
            U = n.n * UNITS + u
            act.wait_ge(M["pt_done"], U + 1)
            wait_for(act, M["pv_done"], U - 1)
            act.activation(probs_t[:, u % 2].rearrange("p j q -> p (j q)"), PT[u % 2][:], ACT.Copy) \
                .then_inc(M["pt_copied"], 1)

        def copy_out_t(n, b):
            act.wait_ge(M["pv_done"], n.n * UNITS + 4 * b + 4)
            wait_for(act, M["o2_done"], n.n * 2 + b - 1)
            act.activation(out_t[:, b].rearrange("p i q -> p (i q)"), PO[:], ACT.Copy).then_inc(M["ot_copied"], 1)

        def input_head(n, a):
            hi, F, t = {"x": (xt_hi, F0, "xt"), "c": (ct_hi, F1, "ct")}[a]
            wait_for(act, M["v_done"], n.n)
            act.wait_ge(M[f"t{a}_done"], (n + 1).n)
            act.activation(hi[:].rearrange("p k b t -> p (k b t)"), F[:], ACT.Copy).then_inc(M[t + "_hi_done"], 1)

        def copy_normed2_t(n):
            act.wait_ge(M["x2t_done"], (n + 1).n)
            wait_for(act, M["rt_done"], n.n)
            act.activation(x2t[:].rearrange("p k b t -> p (k b t)"), F2[:], ACT.Copy).then_inc(M["x2t_copied"], 1)

        def copy_logits_t(n):
            act.wait_ge(M["rt_done"], (n + 1).n)
            wait_for(act, M["lg_done"], n.n)
            act.activation(lt_sb[:], F2[0:64, 0:SEQ], ACT.Copy).then_inc(M["lt_copied"], 1)

        def copy_values(n):
            act.wait_ge(M["v_done"], (n + 1).n)
            act.wait_ge(M["setup_pool"], 2)
            wait_for(act, M["pv_done"], (n - 1).n * UNITS)
            act.activation(v_aug[:, n.par, :, :, 0:DK].rearrange("p b h d -> p (b h) d"),
                           F0[:].rearrange("p (h d) -> p h d", d=DK), ACT.Copy).then_inc(M["v_ready"], 1)

        def attention_head(n):
            act.wait_ge(M["at_done"], (n + 1).n)
            wait_for(act, M["wo_done"], n.n)
            act.activation(at_hi[:].rearrange("p k b t -> p (k b t)"), F1[:], ACT.Copy).then_inc(M["at_hi_done"], 1)

        def query_head(n):
            wait_for(act, M["scores_done"], (n - 1).n * UNITS)
            act.wait_ge(M["q_rotated"], (n + 1).n)
            act.activation(q_hi[:, n.par].rearrange("p k b t -> p (k b t)"),
                           q_rot[:].rearrange("p k t -> p (k t)"), ACT.Copy).then_inc(M["q_hi_done"], 1)

        def key_head(n):
            wait_for(act, M["scores_done"], (n - 1).n * UNITS)
            act.wait_ge(M["k_rotated"], (n + 1).n)
            for e in range(2):
                last = act.activation(k_hi[:, n.par, :, :, e].rearrange("p k b t -> p (k b) t"),
                                      k_rot[:].rearrange("p k (b t) -> p (k b) t", b=2),
                                      ACT.Copy, scale=kmask[:, e:e + 1])
            last.then_inc(M["k_hi_done"], 1)

        def step(s):
            for k in range(UNITS):
                n, u = (s, k - 1) if k else (s - 1, UNITS - 1)
                if n.real:
                    exp_unit(n, u)
                if k == 0 and (s + 1).real:
                    input_head(s + 1, "x")
                if k == 5 and (s + 1).real:
                    copy_values(s + 1)
                if k == 5 and (s - 1).real:
                    attention_head(s - 1)
                n, u = (s, k - 2) if k >= 2 else (s - 1, k + UNITS - 2)
                if n.real:
                    copy_unit(n, u)
                if k == 1 and (s + 1).real:
                    input_head(s + 1, "c")
                if k == 1 and (s - 2).real:
                    copy_normed2_t(s - 2)
                if k == 2 and (s - 1).real:
                    copy_out_t(s - 1, 1)
                if k == 2 and (s - 2).real:
                    copy_logits_t(s - 2)
                if k == 4 and (s + 1).real:
                    query_head(s + 1)
                if k == 5 and (s + 1).real:
                    key_head(s + 1)
                if k == 6 and s.real:
                    copy_out_t(s, 0)
                if s.beyond == 0 and k == 5:
                    early = T["scaled"][:, 0:EARLY].rearrange("p b e -> p (b e)")
                    act.wait_ge(M["soft_step"], 2)
                    act.activation(early, early, ACT.Exp).then_inc(M["soft_exp"], 1)

        run(act, step)

    @block.vector
    def _(dve):
        dve.memset(wr[:, :, EXPERTS:32], 0.0).then_inc(M["setup_dve"], 1)
        dve.wait_ge(M["gate_tanh"], 1)
        dve.tensor_scalar(tb[:], tb[:], gates[:, 2:3], None, ALU.mult).then_inc(M["tb_done"], 1)
        dve.wait_ge(M["w_split"], 1)
        dve.tensor_tensor(w_lo[:].rearrange("p a k e -> p (a k e)"), stage[:].rearrange("p a k e -> p (a k e)"),
                          w_hi[:].rearrange("p a k e -> p (a k e)").bitcast(F32), ALU.subtract).then_inc(M["w_split"], 1)

        def row_max(n, u):
            U = n.n * UNITS + u
            dve.wait_ge(M["scores_done"], U + 1)
            wait_for(dve, M["probs_done"], U - 1)
            dve.sem_inc(M["dve_passed"], 1)
            for j in range(4):
                last = dve.tensor_tensor_reduce(neg_s[:, u % 2, j], S[u % 2][:, j * SEQ:(j + 1) * SEQ], band[:],
                                                1.0, 3e38, ALU.add, ALU.min, neg_max[:, u % 2, j:j + 1])
            last.then_inc(M["rowmax_done"], 1)

        def normalise(n, b):
            dve.wait_ge(M["o2_done"], n.n * 2 + b + 1)
            wait_for(dve, M["at_done"], n.n)
            o2 = F2[:].rearrange("p (h d) -> p h d", d=32)
            dve.reciprocal(rden[:, b], o2[:, :, DK]).then_inc(M["rden_done"], 1)
            dve.wait_ge(M["rden_done"], n.n * 2 + b + 1)
            dve.tensor_tensor(att[:, b].rearrange("p (h d) -> p h d", d=DK), o2[:, :, 0:DK],
                              rden[:, b].rearrange("p (h o) -> p h o", o=1).broadcast_to([P, HEADS, DK]), ALU.mult) \
                .then_inc(M["att_done"], 1)

        def input_rest(n, a):
            hi, lo, F = {"xt": (xt_hi, xt_lo, F0), "ct": (ct_hi, ct_lo, F1)}[a]
            dve.wait_ge(M[a + "_hi_done"], (n + 1).n)
            dve.tensor_tensor(lo[:].rearrange("p k b t -> p (k b t)"), F[:],
                              hi[:].rearrange("p k b t -> p (k b t)").bitcast(F32), ALU.subtract) \
                .then_inc(M[a + "_lo_done"], 1)

        def scale(n, a):
            F, qc, qs = {"q": (F0, q_cos, q_sin), "k": (F1, k_cos, k_sin)}[a]
            dve.wait_ge(M[a + "t_done"], (n + 1).n)
            wait_for(dve, M[a + "_rotated"], n.n)
            for dst, table in ((qc, cos), (qs, sin)):
                last = dve.tensor_tensor(
                    dst[:].rearrange("p k (b t) -> p (k b) t", b=2),
                    F[:].rearrange("p (a t) -> p a t", t=SEQ),
                    table[:].rearrange("p (o t) -> p o t", o=1).broadcast_to([P, 4, SEQ]), ALU.mult)
            last.then_inc(M[a + "_scaled"], 1)

        def norm_stats(n):
            dve.wait_ge(x_in[n.par], n.landed())
            for b in range(2):
                last = dve.bn_stats(stats[:, b], x_in_sb[:, n.par, b])
            last.then_inc(M["ln_stats"], 1)
            dve.wait_ge(M["ln_stats"], (n + 1).n)
            wait_for(dve, M["xn_done"], n.n)
            dve.sem_inc(M["dve_passed"], 1)
            for b in range(2):
                last = dve.bn_aggr(mv[:, b], stats[:, b])
            last.then_inc(M["ln_aggr"], 1)
            dve.wait_ge(M["ln_aggr"], (n + 1).n)
            wait_for(dve, M["rstd_done"], n.n)
            dve.tensor_scalar_add(ve[:], mv[:, :, 1], EPS).then_inc(M["ve_done"], 1)

        def key_rest(n):
            dve.wait_ge(M["k_hi_done"], (n + 1).n)
            for e in range(2):
                last = dve.scalar_tensor_tensor(
                    out=k_lo[:, n.par, :, :, e].rearrange("p k b t -> p (k b) t"),
                    in0=k_rot[:].rearrange("p k (b t) -> p (k b) t", b=2), scalar=kmask[:, e:e + 1],
                    in1=k_hi[:, n.par, :, :, e].rearrange("p k b t -> p (k b) t").bitcast(F32),
                    op0=ALU.mult, op1=ALU.subtract)
            last.then_inc(M["k_lo_done"], 1)

        def attention_rest(n):
            dve.wait_ge(M["at_hi_done"], (n + 1).n)
            dve.tensor_tensor(at_lo[:].rearrange("p k b t -> p (k b t)"), F1[:],
                              at_hi[:].rearrange("p k b t -> p (k b t)").bitcast(F32), ALU.subtract) \
                .then_inc(M["at_lo_done"], 1)

        def residual(n):
            dve.wait_ge(M["wo_done"], (n + 1).n)
            dve.wait_ge(M["xb_done"], (n + 1).n)
            wait_for(dve, x1_out[n.par], (n - 2).landed())
            dve.scalar_tensor_tensor(out=x1[:, n.par].rearrange("p b c -> p (b c)"), in0=F0[:],
                                     scalar=gates[:, 2:3], in1=xb[:].rearrange("p b c -> p (b c)"),
                                     op0=ALU.mult, op1=ALU.add).then_inc(M["x1_done"], 1)

        def residual_stats(n):
            dve.wait_ge(M["x1_done"], (n + 1).n)
            for b in range(2):
                last = dve.bn_stats(stats2[:, b], x1[:, n.par, b])
            last.then_inc(M["ln2_stats"], 1)
            dve.wait_ge(M["ln2_stats"], (n + 1).n)
            dve.sem_inc(M["dve_passed"], 1)
            for b in range(2):
                last = dve.bn_aggr(mv2[:, b], stats2[:, b])
            last.then_inc(M["ln2_aggr"], 1)
            dve.wait_ge(M["ln2_aggr"], (n + 1).n)
            wait_for(dve, M["rstd2_done"], n.n)
            dve.tensor_scalar_add(ve2[:], mv2[:, :, 1], EPS).then_inc(M["ve2_done"], 1)

        def normed2(n):
            dve.wait_ge(M["rstd2_done"], (n + 1).n)
            wait_for(dve, xn2_out[n.par], (n - 2).landed())
            for b in range(2):
                last = dve.tensor_scalar(xn2[:, n.par, b], x1[:, n.par, b], mv2[:, b, 0:1],
                                         rstd2[:, b:b + 1], ALU.subtract, ALU.mult)
            last.then_inc(M["xn2_done"], 1)

        def keep_logits(n):
            dve.wait_ge(M["lg_done"], (n + 1).n)
            dve.tensor_copy(logits[:, bass.ds(n.n * 2, 2), :],
                            F2[:, 256:320].rearrange("p (b e) -> p b e", e=32)[:, :, 0:EXPERTS]) \
                .then_inc(M["logits_done"], 1)

        def early_softmax(part):
            row, early, early_logits = T["row"][:, :, 0:EARLY], T["scaled"][:, 0:EARLY], logits[:, 0:EARLY]

            def per_seq(a):
                return a.rearrange("p (b o) -> p b o", o=1).broadcast_to([P, EARLY, EXPERTS])

            if part == 0:
                dve.wait_ge(M["logits_done"], EARLY // 2)
                dve.tensor_reduce(row[:, 0], early_logits, AX_X, ALU.max).then_inc(M["soft_step"], 1)
            if part == 1:
                dve.wait_ge(M["soft_step"], 1)
                dve.tensor_tensor(early, early_logits, per_seq(row[:, 0]), ALU.subtract).then_inc(M["soft_step"], 1)
            if part == 2:
                dve.wait_ge(M["soft_exp"], 1)
                dve.tensor_reduce(row[:, 1], early, AX_X, ALU.add).then_inc(M["soft_step"], 1)
                dve.wait_ge(M["soft_step"], 3)
                dve.reciprocal(row[:, 2], row[:, 1]).then_inc(M["soft_step"], 1)
            if part == 3:
                dve.wait_ge(M["soft_step"], 4)
                dve.tensor_tensor(early, early, per_seq(row[:, 2]), ALU.mult).then_inc(M["soft_step"], 1)

        def step(s):
            for k in range(UNITS):
                if s.real:
                    row_max(s, k)
                if k == 0 and (s + 1).real:
                    input_rest(s + 1, "xt")
                if k == 0 and (s - 2).real:
                    normed2(s - 2)
                if k == 1 and (s + 2).real:
                    norm_stats(s + 2)
                if k == 1 and (s + 1).real:
                    scale(s + 1, "q")
                if k == 1 and (s + 1).real:
                    input_rest(s + 1, "ct")
                if k == 3 and (s - 2).real:
                    keep_logits(s - 2)
                if k == 3 and (s + 1).real:
                    scale(s + 1, "k")
                if k == 4 and (s - 1).real:
                    normalise(s - 1, 1)
                if k == 5 and (s - 1).real:
                    attention_rest(s - 1)
                if k == 6 and (s + 1).real:
                    key_rest(s + 1)
                if k == 6 and (s - 1).real:
                    residual(s - 1)
                if k == 7 and (s - 1).real:
                    residual_stats(s - 1)
                if k == 7 and s.real:
                    normalise(s, 0)
                if s.beyond == 0 and k == 1:
                    early_softmax(0)
                if s.beyond == 0 and k == 4:
                    early_softmax(1)
                if s.beyond == 0 and k == 6:
                    early_softmax(2)
                if s.beyond == 1 and k == 2:
                    early_softmax(3)

        run(dve, step)

    @block.tensor
    def _(pe):
        pe.wait_ge(M["consts_in"], 16 * 9)
        pe.wait_ge(M["w_split"], 2)
        pe.wait_ge(M["setup_dve"], 1)

        def split_matmul(out, lhs, rhs, first=True, last=True):
            (lh, ll), (rh, rl) = lhs, rhs
            pe.matmul(out, lh, rh, start=first, stop=False)
            pe.matmul(out, ll, rh, start=False, stop=False)
            return pe.matmul(out, lh, rl, start=False, stop=last)

        def scores(n, u):
            b, i = divmod(u, 4)
            U = n.n * UNITS + u
            if u == 0:
                for done in ("q_hi_done", "q_lo_done", "k_hi_done", "k_lo_done"):
                    pe.wait_ge(M[done], (n + 1).n)
            wait_for(pe, M["rowmax_done"], U - 1)
            rows = slice(32 * i, 32 * i + 32)
            for m in range(KC):
                last = split_matmul(S[u % 2][:, m * 2 * SEQ:(m + 1) * 2 * SEQ],
                                    [q[rows, n.par, m, b] for q in (q_hi, q_lo)],
                                    [k[rows, n.par, m, b].rearrange("p e t -> p (e t)") for k in (k_hi, k_lo)])
            last.then_inc(M["scores_done"], 1)

        def transpose_unit(n, u):
            U = n.n * UNITS + u
            pe.wait_ge(M["probs_done"], U + 1)
            wait_for(pe, M["pt_copied"], U - 1)
            for j in range(4):
                last = pe.transpose(PT[u % 2][:, j * SEQ:(j + 1) * SEQ], probs[:, u % 2, j], ident[:])
            last.then_inc(M["pt_done"], 1)

        def values_unit(n, u):
            b, i = divmod(u, 4)
            U = n.n * UNITS + u
            if u == 0:
                pe.wait_ge(M["v_ready"], (n + 1).n)
            pe.wait_ge(M["pt_copied"], U + 1)
            if i == 0:
                wait_for(pe, M["ot_copied"], n.n * 2 + b)
            for j in range(4):
                head = 8 * (j // 2) + 2 * i + j % 2
                last = pe.matmul(PO[32 * j:32 * j + 32, i * SEQ:(i + 1) * SEQ], v_aug[:, n.par, b, head],
                                 probs_t[:, u % 2, j], start=True, stop=True)
            last.then_inc(M["pv_done"], 1)

        def untranspose(n, b):
            pe.wait_ge(M["ot_copied"], n.n * 2 + b + 1)
            for i in range(4):
                last = pe.transpose(F2[:, i * SEQ:(i + 1) * SEQ], out_t[:, b, i], ident[:])
            last.then_inc(M["o2_done"], 1)

        def transposes(F, src):
            for k in range(KC):
                for b in range(2):
                    last = pe.transpose(F[:, (2 * k + b) * SEQ:(2 * k + b + 1) * SEQ], src[:, b, k * P:(k + 1) * P],
                                        ident[:])
            return last

        def project(F, w, hi, lo):
            for m in range(KC):
                for k in range(KC):
                    last = split_matmul(F[:, m * 2 * SEQ:(m + 1) * 2 * SEQ],
                                        [t[:, w, k, m * P:(m + 1) * P] for t in (w_hi, w_lo)],
                                        [t[:, k].rearrange("p b t -> p (b t)") for t in (hi, lo)],
                                        k == 0, k == KC - 1)
            return last

        def apply(F, w, hi, lo):
            for b in range(2):
                for k in range(KC):
                    last = split_matmul(F[:, b * DIM:(b + 1) * DIM], [t[:, k, b] for t in (hi, lo)],
                                        [t[:, w, k] for t in (w_hi, w_lo)], k == 0, k == KC - 1)
            return last

        def inputs_t(n):
            pe.wait_ge(M["xn_done"], (n + 1).n)
            wait_for(pe, M["v_ready"], n.n)
            wait_for(pe, M["x1_done"], (n - 2).n)
            transposes(F0, xn).then_inc(M["tx_done"], 1)

        def context_t(n):
            pe.wait_ge(c_in[n.par], n.landed())
            wait_for(pe, M["k_scaled"], n.n)
            wait_for(pe, M["at_lo_done"], (n - 2).n)
            transposes(F1, c_in_sb[:, n.par]).then_inc(M["tc_done"], 1)

        def normed2_t(n):
            pe.wait_ge(M["xn2_done"], (n + 1).n)
            pe.wait_ge(M["att_done"], (n + 1).n * 2 + 1 if (n + 1).real else 2 * PAIRS)
            transposes(F2, xn2[:, n.par]).then_inc(M["x2t_done"], 1)

        def router(n):
            pe.wait_ge(M["x2t_copied"], (n + 1).n)
            for kk in range(KC):
                for b in range(2):
                    last = pe.matmul(F2[32 * b:32 * b + 32, 0:SEQ], wr[:, kk], x2t[:, kk, b],
                                     start=(kk == 0), stop=(kk == KC - 1))
            last.then_inc(M["rt_done"], 1)

        def logits_t(n):
            pe.wait_ge(M["lt_copied"], (n + 1).n)
            pe.sem_inc(M["pe_passed"], 1)
            pe.transpose(F2[:, 256:320], lt_sb[:], ident[0:64, 0:64]).then_inc(M["lg_done"], 1)

        def input_projection(n, a):
            F, w, hi, lo, t, done = {"q": (F0, 0, xt_hi, xt_lo, "xt", "qt_done"),
                                     "k": (F1, 1, ct_hi, ct_lo, "ct", "kt_done")}[a]
            pe.wait_ge(M[t + "_hi_done"], (n + 1).n)
            pe.wait_ge(M[t + "_lo_done"], (n + 1).n)
            project(F, w, hi, lo).then_inc(M[done], 1)

        def second_untransposed(n):
            wait_for(pe, M["logits_done"], n.n)
            pe.wait_ge(M["att_done"], n.n * 2 + 1)
            untranspose(n, 1)

        def first_untransposed(n):
            wait_for(pe, M["att_done"], n.n * 2)
            untranspose(n, 0)

        def value_projection(n):
            for done in ("ct_hi_done", "ct_lo_done", "q_scaled"):
                pe.wait_ge(M[done], (n + 1).n)
            apply(F0, 2, ct_hi, ct_lo).then_inc(M["v_done"], 1)

        def attention_t(n):
            pe.wait_ge(M["att_done"], n.n * 2 + 2)
            if (n + 2).real:
                pe.wait_ge(M["k_scaled"], (n + 3).n)
            else:
                pe.wait_ge(M["at_lo_done"], n.n)
            transposes(F1, att).then_inc(M["at_done"], 1)

        def output_projection(n):
            pe.wait_ge(M["at_hi_done"], (n + 1).n)
            pe.wait_ge(M["at_lo_done"], (n + 1).n)
            if (n + 2).real:
                pe.wait_ge(M["v_ready"], (n + 3).n)
            else:
                pe.wait_ge(M["x1_done"], n.n)
            apply(F0, 3, at_hi, at_lo).then_inc(M["wo_done"], 1)

        def step(s):
            for k in range(UNITS):
                if k == 0 and (s + 1).real:
                    context_t(s + 1)
                if k == 0 and (s + 1).real:
                    inputs_t(s + 1)
                if s.real:
                    scores(s, k)
                n, u = (s, k - 2) if k >= 2 else (s - 1, k + UNITS - 2)
                if n.real:
                    transpose_unit(n, u)
                if k == 4 and (s - 1).real:
                    second_untransposed(s - 1)
                n, u = (s, k - 3) if k >= 3 else (s - 1, k + UNITS - 3)
                if n.real:
                    values_unit(n, u)
                if k == 1 and (s + 1).real:
                    input_projection(s + 1, "q")
                if k == 1 and (s - 2).real:
                    normed2_t(s - 2)
                if k == 2 and (s - 2).real:
                    router(s - 2)
                if k == 3 and (s - 2).real:
                    logits_t(s - 2)
                if k == 3 and (s + 1).real:
                    input_projection(s + 1, "k")
                if k == 4 and (s + 1).real:
                    value_projection(s + 1)
                if k == 4 and (s - 1).real:
                    attention_t(s - 1)
                if k == 6 and (s - 1).real:
                    output_projection(s - 1)
                if k == 7 and s.real:
                    first_untransposed(s)

        run(pe, step)


def routing_block(nc, ctx, T, D):

    def sb(name, shape, dt=F32):
        return ctx.enter_context(nc.sbuf_tensor(name, shape, dt))

    def sem(name):
        return ctx.enter_context(nc.semaphore(name))

    NB = 32
    BANKS = SEQS // NB
    scaled, row = T["scaled"], T["row"]
    equal = sb("equal", [P, SEQS, EXPERTS])
    chosen = sb("chosen", [P, TOPK, SEQS, EXPERTS], BF16)
    prob = sb("prob", [P, TOPK, SEQS])
    equal_b = sb("equal_b", [P, SEQS, EXPERTS], BF16)
    rev_b = sb("rev_b", [P, EXPERTS], BF16)
    rev_e = sb("rev_e", [P, TOPK, SEQS], BF16)
    expert = sb("expert", [P, TOPK, SEQS])
    rank = sb("rank", [P, TOPK, SEQS])
    gone = sb("gone", [P, TOPK, SEQS])
    kept = sb("kept", [P, TOPK, SEQS])
    rev, before_f = T["rev"], T["before_f"]
    before = sb("before_b", [P, P], BF16)
    ones = sb("ones_b", [P, P], BF16)
    ranks = [ctx.enter_context(nc.psum_tensor(f"ranks{i}", [P, 512], F32)) for i in range(TOPK * BANKS)]
    logits, gates = T["logits"], T["gates"]
    dispatch_slot, collect_slot, weight = T["dispatch_slot"], T["collect_slot"], T["weight"]
    CH = T["chunks"]
    w_hi, w_lo, w_in = [T[w][:].rearrange("p (c n) -> p c n", c=CH) for w in ("we_hi", "we_lo", "w_in")]

    consts2_in = sem("consts2_in")
    heads_done, rests_pool = sem("heads_done"), sem("rests_pool")
    step_done, exp_done, tables_done, ranks_done = sem("step_done"), sem("exp_done"), sem("tables_done"), sem("ranks_done")
    block = ctx.enter_context(nc.Block())

    def per_seq(a):
        return a.rearrange("p (b o) -> p b o", o=1).broadcast_to([P, SEQS, EXPERTS])

    @block.sync
    def _(sp):
        sp.dma_start(T["iota"][:], D["iota_c"]).then_inc(consts2_in, 16)
        sp.dma_start(T["ident2"][:], D["ident"]).then_inc(consts2_in, 16)

    @block.scalar
    def _(act):
        act.wait_ge(step_done, 2)
        late = scaled[:, EARLY:SEQS].rearrange("p b e -> p (b e)")
        act.activation(late, late, ACT.Exp) \
            .then_inc(exp_done, 1)
        act.wait_ge(T["w_landed"], 16 * (2 * KC + 1))
        for c in range(CH):
            act.activation(w_hi[:, c], w_in[:, c], ACT.Copy).then_inc(heads_done, 1)

    @block.gpsimd
    def _(pool):
        for c in range(CH):
            pool.wait_ge(heads_done, c + 1)
            pool.tensor_tensor(w_lo[:, c], w_in[:, c], w_hi[:, c].bitcast(F32), ALU.subtract).then_inc(rests_pool, 1)
        pool.wait_ge(rests_pool, CH)
        pool.wait_ge(consts2_in, 32)

    @block.tensor
    def _(pe):
        pe.wait_ge(tables_done, 2)
        pe.wait_ge(step_done, 10)
        for c in range(BANKS):
            one = chosen[:, 0, c * NB:(c + 1) * NB].rearrange("p b e -> p (b e)")
            pe.matmul(ranks[c][:, 0:NB * EXPERTS], before[:], one, start=True, stop=True)
            last = pe.matmul(ranks[BANKS + c][:, 0:NB * EXPERTS], ones[:], one, start=True, stop=False)
        last.then_inc(ranks_done, 1)
        pe.wait_ge(step_done, 16)
        for c in range(BANKS):
            two = chosen[:, 1, c * NB:(c + 1) * NB].rearrange("p b e -> p (b e)")
            last = pe.matmul(ranks[BANKS + c][:, 0:NB * EXPERTS], before[:], two, start=False, stop=True)
        last.then_inc(ranks_done, 1)

    @block.vector
    def _(dve):
        count = [0]

        def then(instruction):
            count[0] += 1
            instruction.then_inc(step_done, 1)
            dve.wait_ge(step_done, count[0])

        dve.memset(ones[:], 1.0).then_inc(tables_done, 1)
        dve.wait_ge(T["tables_in"], 32)
        dve.tensor_copy(before[:], before_f[:]).then_inc(tables_done, 1)
        dve.tensor_copy(rev_b[:], rev[:]).then_inc(tables_done, 1)
        dve.wait_ge(tables_done, 3)
        late, late_row, late_logits = scaled[:, EARLY:SEQS], row[:, :, EARLY:SEQS], logits[:, EARLY:SEQS]

        def per_late(a):
            return a.rearrange("p (b o) -> p b o", o=1).broadcast_to([P, SEQS - EARLY, EXPERTS])

        then(dve.tensor_reduce(late_row[:, 0], late_logits, AX_X, ALU.max))
        then(dve.tensor_tensor(late, late_logits, per_late(late_row[:, 0]), ALU.subtract))
        dve.wait_ge(exp_done, 1)
        then(dve.tensor_reduce(late_row[:, 1], late, AX_X, ALU.add))
        then(dve.reciprocal(late_row[:, 2], late_row[:, 1]))
        then(dve.tensor_tensor(late, late, per_late(late_row[:, 2]), ALU.mult))
        all_rev = rev_b[:].rearrange("p (o e) -> p o e", o=1).broadcast_to([P, SEQS, EXPERTS])
        for k in range(TOPK):
            then(dve.tensor_reduce(prob[:, k], scaled[:], AX_X, ALU.max))
            then(dve.tensor_tensor(equal_b[:], scaled[:], per_seq(prob[:, k]), ALU.is_equal))
            then(dve.tensor_tensor(equal_b[:], equal_b[:], all_rev, ALU.mult))
            then(dve.tensor_reduce(rev_e[:, k], equal_b[:], AX_X, ALU.max))
            then(dve.tensor_tensor(chosen[:, k], all_rev, per_seq(rev_e[:, k]), ALU.is_equal))
            if k == 0:
                then(dve.scalar_tensor_tensor(out=scaled[:].rearrange("p b e -> p (b e)"),
                                              in0=chosen[:, 0].rearrange("p b e -> p (b e)"), scalar=-4.0,
                                              in1=scaled[:].rearrange("p b e -> p (b e)"),
                                              op0=ALU.mult, op1=ALU.add))
        then(dve.tensor_scalar(weight[:], prob[:], gates[:, 3:4], 0.5, ALU.mult, ALU.mult))
        for k in range(TOPK):
            dve.wait_ge(ranks_done, k + 1)
            for c in range(BANKS):
                last = dve.tensor_tensor(equal[:, c * NB:(c + 1) * NB],
                                         ranks[k * BANKS + c][:, 0:NB * EXPERTS].rearrange("p (b e) -> p b e", e=EXPERTS),
                                         chosen[:, k, c * NB:(c + 1) * NB], ALU.mult)
            then(last)
            then(dve.tensor_reduce(rank[:, k], equal[:], AX_X, ALU.add))
        then(dve.tensor_scalar(expert[:], rev_e[:], -1.0, float(EXPERTS), ALU.mult, ALU.add))
        then(dve.tensor_scalar(gone[:], rank[:], CAP - 0.5, GONE, ALU.is_gt, ALU.mult))
        then(dve.tensor_tensor(gone[:], gone[:], rank[:], ALU.add))
        then(dve.scalar_tensor_tensor(out=dispatch_slot[:], in0=expert[:], scalar=float(CAP), in1=gone[:],
                                      op0=ALU.mult, op1=ALU.add))
        then(dve.tensor_scalar(kept[:], rank[:], CAP - 1.0, float(EXPERTS), ALU.min, ALU.mult))
        then(dve.tensor_tensor(collect_slot[:], kept[:], expert[:], ALU.add))


class Unit:

    def __init__(self, i, c):
        self.i, self.c = i + c // 2, c % 2

    def __sub__(self, d):
        return Unit(self.i, self.c - d)

    @property
    def n(self):
        return self.i * 2 + self.c

    @property
    def group(self):
        return self.i // (GROUP // 2)

    @property
    def j(self):
        return self.i % (GROUP // 2) * 2 + self.c

    @property
    def landed(self):
        return (self.i + 1) * 16


def expert_block(nc, ctx, T, D):
    LOAD, PICK, DISPATCH, SPLIT, GATE, HIDDEN, OUTPUT, FETCH, MIX, COLLECT = -14, -12, -10, -2, 0, 2, 4, 12, 14, 16

    def sb(name, shape, dt=F32):
        return ctx.enter_context(nc.sbuf_tensor(name, shape, dt))

    def sem(name):
        return ctx.enter_context(nc.semaphore(name))

    def pb(name):
        return ctx.enter_context(nc.psum_tensor(name, [P, 512], F32))

    x_in_sb = T["scaled"][:].rearrange("p b e -> p (b e)")[:, 0:4 * DIM].rearrange("p (n c) -> p n c", c=DIM)
    x_hi = sb("x_hi", [P, 2, DIM], F32R)
    x_lo = sb("x_lo", [P, 2, DIM], F32R)
    pick1 = sb("pick1", [P, 2, SLOTS])
    pick = sb("pick", [P, 2, SLOTS], F32R)
    slots = sb("slots", [P, 2, KC, EXPERTS, GROUP, CAP])
    s_hi = sb("s_hi", [P, 2, KC, 2, P], F32R)
    s_lo = sb("s_lo", [P, 2, KC, 2, P], F32R)
    th = sb("th", [P, 2, 2, HID])
    gated = sb("gated", [P, 2, HID])
    hid = sb("hid", [P, 2, 2, HID])
    h_hi = sb("h_hi", [P, 2, 2, P], F32R)
    h_lo = sb("h_lo", [P, 2, 2, P], F32R)
    eo = sb("eo", [P, 2, 2, DIM])
    e_in = sb("e_in", [P, 2, 2, DIM])
    e_hi = sb("e_hi", [P, 2, 2, DIM], F32R)
    e_lo = sb("e_lo", [P, 2, 2, DIM], F32R)
    mix1 = sb("mix1", [P, SLOTS])
    mix2 = sb("mix2", [P, SLOTS])
    mix = sb("mix", [P, 2, SLOTS])
    m_hi = sb("m_hi", [P, 2, 2, P], F32R)
    m_lo = sb("m_lo", [P, 2, 2, P], F32R)
    xr = sb("xr", [P, 4, DIM])
    y_sb = sb("y_sb", [P, 2, DIM])
    ident, iota = T["ident2"], T["iota"]
    dispatch_slot, collect_slot, weight = T["dispatch_slot"], T["collect_slot"], T["weight"]
    half = EXPERTS * 2 * HID
    w_gu = [T[w][:, 0:KC * half].rearrange("p (k n) -> p k n", k=KC) for w in ("we_hi", "we_lo")]
    w_down = [T[w][:, KC * half:] for w in ("we_hi", "we_lo")]

    names = ("x_hi_done x_lo_done pick1_done pick_done ds_done slots_done s_hi_done s_lo_done gu_done th_done "
             "gated_done hid_done ht_done h_hi_done h_lo_done eo_done eo_copied e_hi_done e_lo_done mix12_done "
             "mix_done mt_done m_hi_done m_lo_done y_done out_done").split()
    M = {n: sem(n) for n in names}
    x_in = [sem("xn2_in0"), sem("xn2_in1")]
    e_landed = [sem("e_in0"), sem("e_in1")]
    x1_in = [sem("x1_in0"), sem("x1_in1")]
    eo_out = [sem("eo_out0"), sem("eo_out1")]
    y_out = [sem("y_out0"), sem("y_out1")]
    DS = [pb("DS0"), pb("DS1")]
    HT, EO, MT, Y = pb("HT"), pb("EOB"), pb("MT"), pb("Y")
    GU = [pb("GU0"), pb("GU1")]
    block = ctx.enter_context(nc.Block())

    def run(eng, step):
        lags = (LOAD, PICK, DISPATCH, SPLIT, GATE, HIDDEN, OUTPUT, FETCH, MIX, COLLECT)
        cuts = sorted({e + x for x in lags for e in (0, 2, SEQS)})
        for a, b in zip(cuts, cuts[1:]):
            def on(lag):
                return lag <= a and b <= SEQS + lag
            if b - a <= 2:
                for u in range(a, b):
                    step(lambda lag: Unit(0, u - lag), on)
            else:
                with eng.Fori((a - LOAD) // 2, (b - LOAD) // 2) as i:
                    for c in range(2):
                        step(lambda lag: Unit(i, c - (lag - LOAD)), on)

    def flat(a):
        return a.rearrange("p a b -> p (a b)")

    @block.sync
    def _(sp):
        def step(unit, on):
            n = unit(COLLECT)
            if on(COLLECT):
                sp.wait_ge(M["out_done"], n.n + 1)
                sp.dma_start(D["out"][bass.ds(n.n, 1)].rearrange("b t c -> t b c"), y_sb[:, n.c:n.c + 1]) \
                    .then_inc(y_out[n.c], 16)
            n = unit(LOAD)
            if on(LOAD):
                wait_for(sp, M["x_hi_done"], n.n - 1)
                sp.dma_start(x_in_sb[:, bass.ds(n.n % 4, 1)], D["xn2_d"][:, bass.ds(n.n, 1)]).then_inc(x_in[n.c], 16)
            n = unit(OUTPUT)
            if on(OUTPUT):
                sp.wait_ge(M["eo_copied"], n.n + 1)
                sp.dma_start(D["eo_d"][bass.ds(n.group * P, P), bass.ds(n.j * 2, 2)], eo[:, n.c]) \
                    .then_inc(eo_out[n.c], 16)
            n = unit(FETCH)
            if on(FETCH):
                for q in eo_out:
                    sp.wait_ge(q, (n.group + 1) * (GROUP // 2) * 16)
                wait_for(sp, M["e_lo_done"], n.n - 1)
                sp.dma_start(e_in[:, n.c], D["eo_d"][bass.ds(n.n * CAP, CAP)]
                             .rearrange("r e c -> (r e) c").rearrange("(h p) c -> p h c", h=2)).then_inc(e_landed[n.c], 16)
                wait_for(sp, M["out_done"], n.n - 3)
                sp.dma_start(xr[:, bass.ds(n.n % 4, 1)], D["x1_d"][:, bass.ds(n.n, 1)]).then_inc(x1_in[n.c], 16)

        run(sp, step)
        for q in y_out:
            sp.wait_ge(q, 16 * (SEQS // 2))

    @block.gpsimd
    def _(pool):
        def step(unit, on):
            n = unit(MIX)
            if on(MIX):
                pool.wait_ge(M["e_hi_done"], n.n + 1)
                wait_for(pool, M["y_done"], n.n - 1)
                pool.tensor_tensor(flat(e_lo[:, n.c]), flat(e_in[:, n.c]), flat(e_hi[:, n.c]).bitcast(F32),
                                   ALU.subtract).then_inc(M["e_lo_done"], 1)
            n = unit(PICK)
            if on(PICK):
                pool.wait_ge(M["x_hi_done"], n.n + 1)
                wait_for(pool, M["ds_done"], n.n - 1)
                pool.tensor_tensor(x_lo[:, n.c:n.c + 1], x_in_sb[:, bass.ds(n.n % 4, 1)],
                                   x_hi[:, n.c:n.c + 1].bitcast(F32), ALU.subtract) \
                    .then_inc(M["x_lo_done"], 1)
            n = unit(SPLIT)
            if on(SPLIT):
                pool.wait_ge(M["s_hi_done"], n.n + 1)
                wait_for(pool, M["gu_done"], n.n - 1)
                src = slots[:, bass.ds(n.group % 2, 1), :, bass.ds(n.j * 2, 2)].rearrange("p o k e b s -> p (o k) e (b s)")
                pool.tensor_tensor(s_lo[:, n.c], src, s_hi[:, n.c].bitcast(F32), ALU.subtract) \
                    .then_inc(M["s_lo_done"], 1)

        run(pool, step)

    @block.scalar
    def _(act):
        def step(unit, on):
            n = unit(MIX)
            if on(MIX):
                act.wait_ge(M["mt_done"], n.n + 1)
                wait_for(act, M["y_done"], n.n - 1)
                act.activation(flat(m_hi[:, n.c]), MT[:, 0:2 * P], ACT.Copy).then_inc(M["m_hi_done"], 1)
                act.wait_ge(e_landed[n.c], n.landed)
                act.activation(flat(e_hi[:, n.c]), flat(e_in[:, n.c]), ACT.Copy).then_inc(M["e_hi_done"], 1)
            n = unit(OUTPUT)
            if on(OUTPUT):
                act.wait_ge(M["eo_done"], n.n + 1)
                wait_for(act, eo_out[n.c], (n - 2).landed)
                act.activation(flat(eo[:, n.c]), EO[:], ACT.Copy).then_inc(M["eo_copied"], 1)
            n = unit(HIDDEN)
            if on(HIDDEN):
                act.wait_ge(M["ht_done"], n.n + 1)
                wait_for(act, M["eo_done"], n.n - 1)
                act.activation(flat(h_hi[:, n.c]), HT[:, 0:2 * P], ACT.Copy).then_inc(M["h_hi_done"], 1)
            n = unit(PICK)
            if on(PICK):
                act.wait_ge(x_in[n.c], n.landed)
                wait_for(act, M["ds_done"], n.n - 1)
                act.activation(x_hi[:, n.c:n.c + 1], x_in_sb[:, bass.ds(n.n % 4, 1)], ACT.Copy).then_inc(M["x_hi_done"], 1)
            n = unit(GATE)
            if on(GATE):
                act.wait_ge(M["gu_done"], n.n + 1)
                wait_for(act, M["gated_done"], n.n - 1)
                act.activation(th[:, n.c], GU[n.c][:].rearrange("p (e f n) -> p e f n", e=2, f=2)[:, :, 0],
                               ACT.Tanh, scale=0.5).then_inc(M["th_done"], 1)
            n = unit(SPLIT)
            if on(SPLIT):
                act.wait_ge(M["slots_done"], (n.group + 1) * GROUP)
                wait_for(act, M["gu_done"], n.n - 1)
                src = slots[:, bass.ds(n.group % 2, 1), :, bass.ds(n.j * 2, 2)].rearrange("p o k e b s -> p (o k) e (b s)")
                act.activation(s_hi[:, n.c], src, ACT.Copy).then_inc(M["s_hi_done"], 1)
            n = unit(DISPATCH)
            if on(DISPATCH):
                act.wait_ge(M["ds_done"], n.n + 1)
                if on(SPLIT):
                    wait_for(act, M["s_lo_done"], n.n - GROUP)
                dst = slots[:, bass.ds(n.group % 2, 1), :, :, bass.ds(n.j, 1)] \
                    .rearrange("p o k e b s -> p (o k) e (b s)")
                act.activation(dst, DS[n.c][:].rearrange("p (k e s) -> p k e s", k=KC, s=CAP), ACT.Copy) \
                    .then_inc(M["slots_done"], 1)

        run(act, step)

    @block.vector
    def _(dve):
        def step(unit, on):
            n = unit(PICK)
            if on(PICK):
                wait_for(dve, M["pick_done"], n.n - 1)
                dve.tensor_scalar(pick1[:, n.c], iota[:], dispatch_slot[:, 0, bass.ds(n.n, 1)], None, ALU.is_equal) \
                    .then_inc(M["pick1_done"], 1)
            n = unit(COLLECT)
            if on(COLLECT):
                dve.wait_ge(M["y_done"], n.n + 1)
                dve.wait_ge(x1_in[n.c], n.landed)
                wait_for(dve, y_out[n.c], (n - 2).landed)
                dve.tensor_tensor(y_sb[:, n.c:n.c + 1], Y[:, 0:DIM].rearrange("p (o c) -> p o c", o=1),
                                  xr[:, bass.ds(n.n % 4, 1)], ALU.add).then_inc(M["out_done"], 1)
            n = unit(MIX)
            if on(MIX):
                dve.wait_ge(M["m_hi_done"], n.n + 1)
                wait_for(dve, M["y_done"], n.n - 1)
                dve.tensor_tensor(flat(m_lo[:, n.c]), MT[:, 0:2 * P], flat(m_hi[:, n.c]).bitcast(F32), ALU.subtract) \
                    .then_inc(M["m_lo_done"], 1)
            n = unit(FETCH)
            if on(FETCH):
                wait_for(dve, M["mix_done"], n.n)
                for dst, k in ((mix1, 0), (mix2, 1)):
                    last = dve.tensor_scalar(dst[:], iota[:], collect_slot[:, k, bass.ds(n.n, 1)],
                                             weight[:, k, bass.ds(n.n, 1)], ALU.is_equal, ALU.mult)
                last.then_inc(M["mix12_done"], 1)
            n = unit(HIDDEN)
            if on(HIDDEN):
                dve.wait_ge(M["h_hi_done"], n.n + 1)
                wait_for(dve, M["eo_done"], n.n - 1)
                dve.tensor_tensor(flat(h_lo[:, n.c]), HT[:, 0:2 * P], flat(h_hi[:, n.c]).bitcast(F32), ALU.subtract) \
                    .then_inc(M["h_lo_done"], 1)
            n = unit(GATE)
            if on(GATE):
                gu = GU[n.c][:].rearrange("p (e f n) -> p e f n", e=2, f=2)
                dve.wait_ge(M["th_done"], n.n + 1)
                wait_for(dve, M["hid_done"], n.n)
                dve.scalar_tensor_tensor(out=gated[:], in0=th[:, n.c], scalar=1.0, in1=gu[:, :, 0],
                                         op0=ALU.add, op1=ALU.mult).then_inc(M["gated_done"], 1)
                dve.wait_ge(M["gated_done"], n.n + 1)
                wait_for(dve, M["ht_done"], n.n - 1)
                dve.tensor_tensor(hid[:, n.c], gated[:], gu[:, :, 1], ALU.mult).then_inc(M["hid_done"], 1)
            n = unit(FETCH)
            if on(FETCH):
                dve.wait_ge(M["mix12_done"], n.n + 1)
                wait_for(dve, M["mt_done"], n.n - 1)
                dve.tensor_tensor(mix[:, n.c], mix1[:], mix2[:], ALU.add).then_inc(M["mix_done"], 1)
            n = unit(PICK)
            if on(PICK):
                dve.wait_ge(M["pick1_done"], n.n + 1)
                wait_for(dve, M["ds_done"], n.n - 1)
                dve.scalar_tensor_tensor(out=pick[:, n.c], in0=iota[:], scalar=dispatch_slot[:, 1, bass.ds(n.n, 1)],
                                         in1=pick1[:, n.c], op0=ALU.is_equal, op1=ALU.add) \
                    .then_inc(M["pick_done"], 1)

        run(dve, step)

    @block.tensor
    def _(pe):
        def split_matmul(out, lhs, rhs, first=True, last=True):
            (lh, ll), (rh, rl) = lhs, rhs
            pe.matmul(out, lh, rh, start=first, stop=False)
            pe.matmul(out, ll, rh, start=False, stop=False)
            return pe.matmul(out, lh, rl, start=False, stop=last)

        def step(unit, on):
            n = unit(DISPATCH)
            if on(DISPATCH):
                pe.wait_ge(M["pick_done"], n.n + 1)
                pe.wait_ge(M["x_hi_done"], n.n + 1)
                pe.wait_ge(M["x_lo_done"], n.n + 1)
                wait_for(pe, M["slots_done"], n.n - 1)
                for k in range(KC):
                    out = DS[n.c][:, k * SLOTS:(k + 1) * SLOTS]
                    pe.matmul(out, x_hi[:, n.c, k * P:(k + 1) * P], pick[:, n.c], start=True, stop=False)
                    last = pe.matmul(out, x_lo[:, n.c, k * P:(k + 1) * P], pick[:, n.c], start=False, stop=True)
                last.then_inc(M["ds_done"], 1)
            n = unit(COLLECT)
            if on(COLLECT):
                for done in ("e_hi_done", "e_lo_done", "m_hi_done", "m_lo_done"):
                    pe.wait_ge(M[done], n.n + 1)
                wait_for(pe, M["out_done"], n.n)
                for h in range(2):
                    last = split_matmul(Y[:, 0:DIM], [m[:, n.c, h] for m in (m_hi, m_lo)],
                                        [e[:, n.c, h] for e in (e_hi, e_lo)], h == 0, h == 1)
                last.then_inc(M["y_done"], 1)
            n = unit(MIX)
            if on(MIX):
                pe.wait_ge(M["mix_done"], n.n + 1)
                wait_for(pe, M["m_lo_done"], n.n)
                for h in range(2):
                    last = pe.transpose(MT[:, h * P:(h + 1) * P], mix[:, n.c, h * P:(h + 1) * P], ident[:])
                last.then_inc(M["mt_done"], 1)

            n = unit(OUTPUT)
            if on(OUTPUT):
                for done in ("h_hi_done", "h_lo_done"):
                    pe.wait_ge(M[done], n.n + 1)
                wait_for(pe, M["eo_copied"], n.n)
                for e in range(2):
                    last = split_matmul(EO[:, e * DIM:(e + 1) * DIM], [h[:, n.c, e] for h in (h_hi, h_lo)],
                                        [w[:, bass.ds(n.j * (2 * DIM) + e * DIM, DIM)] for w in w_down])
                last.then_inc(M["eo_done"], 1)
            n = unit(HIDDEN)
            if on(HIDDEN):
                pe.wait_ge(M["hid_done"], n.n + 1)
                wait_for(pe, M["h_lo_done"], n.n)
                for e in range(2):
                    last = pe.transpose(HT[:, e * P:(e + 1) * P], hid[:, n.c, e], ident[:])
                last.then_inc(M["ht_done"], 1)
            n = unit(GATE)
            if on(GATE):
                for done in ("s_hi_done", "s_lo_done"):
                    pe.wait_ge(M[done], n.n + 1)
                wait_for(pe, M["hid_done"], n.n - 1)
                for e in range(2):
                    for k in range(KC):
                        last = split_matmul(GU[n.c][:, e * 2 * HID:(e + 1) * 2 * HID],
                                            [t[:, n.c, k, e] for t in (s_hi, s_lo)],
                                            [w[:, k, bass.ds(n.j * (4 * HID) + e * 2 * HID, 2 * HID)] for w in w_gu],
                                            k == 0, k == KC - 1)
                last.then_inc(M["gu_done"], 1)

        run(pe, step)


def flamingo_kernel(nc, D):
    with ExitStack() as outer:
        def sb(name, shape, dt=F32):
            return outer.enter_context(nc.sbuf_tensor(name, shape, dt))

        D["x1_d"] = nc.dram_tensor("x1_d", [P, SEQS, DIM], F32).ap()
        D["xn2_d"] = nc.dram_tensor("xn2_d", [P, SEQS, DIM], F32).ap()
        D["eo_d"] = nc.dram_tensor("eo_d", [SEQS * CAP, EXPERTS, DIM], F32).ap()
        T = {"gates": sb("gates", [P, 4]), "logits": sb("logits", [P, SEQS, EXPERTS])}
        size = KC * EXPERTS * 2 * HID + EXPERTS * DIM
        T["chunks"] = size // 1024
        T["scaled"] = sb("scaled", [P, SEQS, EXPERTS])
        T["row"] = sb("row", [P, 3, SEQS])
        T["rev"], T["before_f"] = sb("rev_sb", [P, EXPERTS]), sb("before_f", [P, P])
        T["tables_in"] = outer.enter_context(nc.semaphore("tables_in"))
        T["w_landed"] = outer.enter_context(nc.semaphore("w_landed"))
        T["iota"], T["ident2"] = sb("iota_sb", [P, SLOTS]), sb("ident2", [P, P])
        with ExitStack() as ctx:
            T["w_in"] = ctx.enter_context(nc.sbuf_tensor("w_in", [P, size], F32))
            attention_block(nc, ctx, T, D)
        T["we_lo"] = sb("we_lo", [P, size], F32R)
        T["we_hi"] = sb("we_hi", [P, size], F32R)
        for name in ("dispatch_slot", "collect_slot", "weight"):
            T[name] = sb(name, [P, TOPK, SEQS])
        with ExitStack() as ctx:
            routing_block(nc, ctx, T, D)
        with ExitStack() as ctx:
            expert_block(nc, ctx, T, D)


def kernel(**inputs):
    import concourse.bacc as bacc
    from concourse.bass_utils import run_bass_kernel_spmd

    a = {k: np.ascontiguousarray(v) for k, v in inputs.items()}
    wo = np.ascontiguousarray(
        a["L0_xattn_wo_w"].T.reshape(KC, 4, 2, DK, DIM).transpose(1, 0, 2, 3, 4).reshape(DIM, DIM))
    inv_freq = (1.0 / 10000.0 ** (np.arange(P, dtype=np.float32) / np.float32(P))).astype(np.float32)
    angle = inv_freq[:, None] * np.arange(SEQ, dtype=np.float32)[None, :]
    at = np.arange(P)
    arrays = {
        "x": a["x"], "ctx": a["ctx_1024"], "g_xattn": a["g_xattn"], "g_ffn": a["g_ffn"],
        "wq": np.ascontiguousarray(a["L0_xattn_wq"].T), "wk": np.ascontiguousarray(a["L0_xattn_wk"].T),
        "wv": np.ascontiguousarray(a["L0_xattn_wv"].T), "wo": wo, "wo_b": a["L0_xattn_wo_b"],
        "w_router": a["L0_ffn_w_router"], "w_fc": a["L0_ffn_w_fc"], "w_gate": a["L0_ffn_w_gate"],
        "w_proj": a["L0_ffn_w_proj"],
        "cos": np.cos(angle).astype(np.float32), "sin": np.sin(angle).astype(np.float32),
        "band": np.where(np.abs(at[:, None] - at[None, :]) <= WINDOW, 0.0, FAR).astype(np.float32),
        "kmask": np.stack([np.where(at // DK % 2 == e, -float(DK) ** 0.5, 0.0) for e in range(2)], 1).astype(np.float32),
        "ident": np.eye(P, dtype=np.float32),
        "rev": np.broadcast_to(EXPERTS - np.arange(EXPERTS, dtype=np.float32), (P, EXPERTS)).copy(),
        "before": (at[:, None] < at[None, :]).astype(np.float32),
        "iota_c": np.broadcast_to(np.arange(SLOTS, dtype=np.float32), (P, SLOTS)).copy(),
    }
    nc = bacc.Bacc("TRN2", target_bir_lowering=False, num_devices=1)
    D = {n: nc.dram_tensor(n, v.shape, F32, kind="ExternalInput").ap() for n, v in arrays.items()}
    D["out"] = nc.dram_tensor("out", [SEQS, SEQ, DIM], F32, kind="ExternalOutput").ap()
    flamingo_kernel(nc, D)
    r = run_bass_kernel_spmd(nc, [arrays], core_ids=[0])
    return r.results[0]["out"]
```
